# Optimizing a Trainium2 kernel written in Bass

```python
import numpy as np
import jax
import jax.numpy as jnp

def _softmax(x, axis=-1):
    return jax.nn.softmax(x, axis=axis)
def _gelu(x):
    return jax.nn.gelu(x, approximate=True)
def _silu(x):
    return jax.nn.silu(x)
def _sigmoid(x):
    return jax.nn.sigmoid(x)
def _layernorm(x, axis=-1, eps=1e-5):
    m = jnp.mean(x, axis=axis, keepdims=True)
    v = jnp.var(x, axis=axis, keepdims=True)
    return (x - m) / jnp.sqrt(v + eps)
def _scatter_add(tgt, idx, src, axis=0):
    return tgt.at[idx].add(src)
def _segment_sum(src, seg, n):
    return jax.ops.segment_sum(src, seg, n)

kernel_name = 'mk_adj_preln_d1_adj_256_747664'

def setup_inputs(seed: int = 0):
    np.random.seed(seed)
    _w = jnp.asarray
    def _rec_inputs():
        import jax
        import jax.numpy as jnp
        _gk = jax.random.key(seed)
        x = -0.0005207 + 1.001 * jax.random.normal(jax.random.fold_in(_gk, 1), (8192, 256), jnp.float32)
        _a = jax.random.bernoulli(jax.random.fold_in(_gk, 2), 0.00195312, (8192, 8192))
        _a = jnp.logical_or(_a, jnp.swapaxes(_a, -1, -2))
        _a = jnp.logical_or(_a, jnp.eye(8192, dtype=bool))
        adj = _a.astype(jnp.int32)
        return x, adj
    x, adj = _rec_inputs()
    def _L0_gnn_setup():
        import jax, jax.numpy as jnp
        import numpy as np
        N, D, H = (8192, 256, 128)
        NEG_BIG = -1000000000.0
        LEAKY_SLOPE = 0.01
        key = jax.random.key(seed)
        ks = jax.random.split(key, 6)
        inlayer = jax.random.normal(ks[0], (N, D), jnp.float32)
        inlayer2 = jax.random.normal(ks[1], (N, D), jnp.float32)
        adj_mat = jax.random.randint(ks[2], (N, N), 0, 2, jnp.int32)
        W = jax.random.uniform(ks[3], (H, D), jnp.float32, -1.0, 1.0) * np.float32(np.sqrt(6.0 / (D + H)))
        b = jnp.zeros((H,), jnp.float32)
        w1 = jax.random.uniform(ks[4], (H,), jnp.float32, -1.0, 1.0) * np.float32(np.sqrt(6.0 / (H + 1)))
        b1 = jnp.zeros((1,), jnp.float32)
        w2 = jax.random.uniform(ks[5], (H,), jnp.float32, -1.0, 1.0) * np.float32(np.sqrt(6.0 / (H + 1)))
        b2 = jnp.zeros((1,), jnp.float32)
        return {'inlayer': inlayer, 'inlayer2': inlayer2, 'adj_mat': adj_mat, 'W': W, 'b': b, 'w1': w1, 'b1': b1, 'w2': w2, 'b2': b2}
    _L0_gnn_all = _L0_gnn_setup()
    _L0_gnn_in = {k: v for k, v in _L0_gnn_all.items() if k in ('inlayer2', 'W', 'b', 'w1', 'b1', 'w2', 'b2', )}
    del _L0_gnn_all

    return {
        "x": x,
        "adj": adj,
        "L0_gnn_inlayer2": _L0_gnn_in["inlayer2"],
        "L0_gnn_W": _L0_gnn_in["W"],
        "L0_gnn_b": _L0_gnn_in["b"],
        "L0_gnn_w1": _L0_gnn_in["w1"],
        "L0_gnn_b1": _L0_gnn_in["b1"],
        "L0_gnn_w2": _L0_gnn_in["w2"],
        "L0_gnn_b2": _L0_gnn_in["b2"],
    }

def reference(x, adj, L0_gnn_inlayer2, L0_gnn_W, L0_gnn_b, L0_gnn_w1, L0_gnn_b1, L0_gnn_w2, L0_gnn_b2):
    import jax
    import jax.numpy as jnp
    def _L0_gnn_ref(inlayer, inlayer2, adj_mat, W, b, w1, b1, w2, b2):
        import jax, jax.numpy as jnp
        import numpy as np
        N, D, H = (8192, 256, 128)
        NEG_BIG = -1000000000.0
        LEAKY_SLOPE = 0.01
        h = inlayer2 @ W.T + b
        f1 = h @ w1 + b1
        f2 = h @ w2 + b2
        logits = f1[:, None] + f2[None, :]
        bias_mat = NEG_BIG * (1.0 - (adj_mat > 0).astype(jnp.float32))
        coefs = jax.nn.softmax(jax.nn.leaky_relu(logits, LEAKY_SLOPE) + bias_mat, axis=-1)
        vals = coefs @ inlayer
        return vals

    h = jnp.maximum(_layernorm(x, axis=-1), 0.0)
    x = x + _L0_gnn_ref(h, L0_gnn_inlayer2, adj, L0_gnn_W, L0_gnn_b, L0_gnn_w1, L0_gnn_b1, L0_gnn_w2, L0_gnn_b2)
    return x


_drawn_inputs = setup_inputs


def setup_inputs(seed=0):
    import zlib

    import numpy as np

    out = dict(_drawn_inputs(seed))
    spreads = {'L0_gnn_b': (0.0, 0.657)}
    factors = {}
    for name, (base, spread) in spreads.items():
        noise = np.random.default_rng([zlib.crc32(name.encode()), seed]).standard_normal(out[name].shape)
        drawn = base * np.exp(spread * noise) if base else spread * noise
        out[name] = jnp.asarray(drawn.astype(out[name].dtype))
    for name, factor in factors.items():
        out[name] = (out[name] * factor).astype(out[name].dtype)
    return out
```

```python
from contextlib import ExitStack

import concourse.bass as bass
from concourse import mybir

ALU = mybir.AluOpType
ACT = mybir.ActivationFunctionType
AX = mybir.AxisListType
F32 = mybir.dt.float32
F16 = mybir.dt.float16
BF16 = mybir.dt.bfloat16
I32 = mybir.dt.int32

P = 128
SLOPE = 0.01
EPS = 1e-5
H_SCALE = 2048.0


def graph_attention(nc, x, adj, inlayer2, W, b, w1, b1, w2, b2, out):
    N, D = x.shape
    HID = W.shape[0]
    assert HID == P and D == 2 * P and N % 2048 == 0
    ROWS = N // P
    CHUNK = 2048
    NC = N // CHUNK
    STRIP = 1024
    NS = N // STRIP
    TS = STRIP // P
    PER = CHUNK // STRIP
    DV = D + 1
    DVP = D + 2
    HD = D // P
    assert NC == 4 and PER == 2 and NS == 8

    adj_rows = adj.rearrange("(i p) (c n) -> i p c n", p=P, n=CHUNK)
    x_rows = x.rearrange("(i p) d -> i p d", p=P)
    out_rows = out.rearrange("(i p) d -> i p d", p=P)
    x_strips = x.rearrange("(q t p) d -> q p t d", p=P, t=TS)
    in2_strips = inlayer2.rearrange("(q t p) d -> q p t d", p=P, t=TS)

    with ExitStack() as ctx:
        def sb(name, shape, dt):
            return ctx.enter_context(nc.sbuf_tensor(name, shape, dt))

        def sem(name):
            return ctx.enter_context(nc.semaphore(name))

        b_all = sb("b_all", [P, N], F32)
        H = sb("H", [P, ROWS, 2, DVP], F16)
        adj_sb = sb("adj_sb", [P, NC, CHUNK], I32)
        wgt = sb("wgt", [P, NC, CHUNK], F32)
        p_hi = sb("p_hi", [P, 2, STRIP], F16)
        p_lo = sb("p_lo", [P, 2, STRIP], BF16)
        x_res = sb("x_res", [P, 2, D], F32)
        o_sb = sb("o_sb", [P, 2, D], F32)
        ident = sb("ident", [P, P], F32)
        in2T = sb("in2T", [P, 2, HD, STRIP], F32)
        W_sb = sb("W_sb", [P, D], F32)
        w12 = sb("w12", [P, 2], F32)
        b_col = sb("b_col", [P, 1], F32)
        b12 = sb("b12", [1, 2], F32)
        ones = sb("ones", [P, P], F32)
        b_rep = sb("b_rep", [P, P], F32)
        U = sb("U", [P, HD, 2], F32)
        U2_rep = sb("U2_rep", [P, HD, P], F32)
        cst = sb("cst", [P, 2], F32)
        f_col = sb("f_col", [P, ROWS, 2], F32)
        stats = sb("stats", [P, ROWS, 6], F32)
        mv = sb("mv", [P, ROWS, 2], F32)
        f2_max = sb("f2_max", [P, NS], F32)
        tiny = sb("tiny", [P, 8], F32)
        t_row = sb("t_row", [P, ROWS], F32)
        low = sb("low", [P, 2, ROWS], F32)
        g_row = sb("g_row", [P, ROWS], F32)
        c_row = sb("c_row", [P, ROWS], F32)
        neg_c = sb("neg_c", [P, ROWS], F32)
        sdev = sb("sdev", [P, ROWS], F32)
        rstd = sb("rstd", [P, ROWS], F32)
        D_col = sb("D_col", [P, ROWS], F32)
        D_inv = sb("D_inv", [P, ROWS], F32)
        D_big = sb("D_big", [P, ROWS], F32)
        h_mul = sb("h_mul", [P, ROWS], F32)
        h_add = sb("h_add", [P, ROWS], F32)
        h_sum = sb("h_sum", [1, D], F32)
        h_mean = sb("h_mean", [P, D], F32)
        no_nb = sb("no_nb", [P, 2], F32)
        den = sb("den", [P, 2], F32)
        r_den = sb("r_den", [P, 2], F32)

        tp = ctx.enter_context(nc.psum_tensor("tp", [P, 2, STRIP], F32))
        acc = ctx.enter_context(nc.psum_tensor("acc", [P, 2, 512], F32))
        small = ctx.enter_context(nc.psum_tensor("small", [P, 2, 512], F32))
        f2_ps = acc[:, :, :].rearrange("p a n -> p (a n)")
        fc_ps = small[:, 0, 0:2 * ROWS]
        cst_ps = small[:, 1, 0:2]
        U_ps = small[:, 1, 2:2 + 2 * HD]
        hs_ps = small[0:1, 1, 0:D]
        hm_ps = small[:, 0, 0:D]

        def in2_stage(q):
            return wgt[:, q % NC, :].rearrange("p (t d) -> p t d", d=D)

        def x_stage(q):
            slot = adj_sb[:, q, :].bitcast(F32) if q < NC else wgt[:, q - NC, :]
            return slot.rearrange("p (t d) -> p t d", d=D)

        small_loaded = sem("small_loaded")
        in2_loaded = [sem(f"in2_loaded{i}") for i in range(NC)]
        xs_loaded = [sem(f"xs_loaded{i}") for i in range(NS)]
        ident_zero = sem("ident_zero")
        ident_ready = sem("ident_ready")
        ones_ready = sem("ones_ready")
        b_rep_ready = sem("b_rep_ready")
        u_ps_ready = sem("u_ps_ready")
        u_ready = sem("u_ready")
        in2T_ps_ready = sem("in2T_ps_ready")
        in2T_act = sem("in2T_act")
        in2T_dve = sem("in2T_dve")
        f2_ps_ready = sem("f2_ps_ready")
        f_strip_done = sem("f_strip_done")
        f2_copied = sem("f2_copied")
        dve_step = sem("dve_step")
        f_max_ready = sem("f_max_ready")
        sdev_ready = sem("sdev_ready")
        exps_ready = sem("exps_ready")
        var_ready = sem("var_ready")
        rows_low = sem("rows_low")
        h_affine_ready = sem("h_affine_ready")
        h_ready = sem("h_ready")
        hi_ready = sem("hi_ready")
        lo_ready = sem("lo_ready")
        h_sum_ps_ready = sem("h_sum_ps_ready")
        h_sum_ready = sem("h_sum_ready")
        h_mean_ps_ready = sem("h_mean_ps_ready")
        h_mean_ready = sem("h_mean_ready")
        d_cols_ready = sem("d_cols_ready")
        rows_ready = sem("rows_ready")
        adj_loaded = [sem(f"adj_loaded{c}") for c in range(NC)]
        r_ready = sem("r_ready")
        p_ready = sem("p_ready")
        t_ready = sem("t_ready")
        hi_split = sem("hi_split")
        lo_split = sem("lo_split")
        mm_done = sem("mm_done")
        x_loaded = [sem(f"x_loaded{i}") for i in range(2)]
        fin_step = sem("fin_step")
        acc_read = sem("acc_read")
        o_ready = sem("o_ready")
        o_stored = [sem(f"o_stored{i}") for i in range(2)]

        def row_tiles(eng, body):
            body(0, 0, 0)
            with eng.Fori(0, ROWS // 2 - 1) as v:
                body(2 * v + 1, 1, v)
                body(2 * v + 2, 0, v + 1)
            body(ROWS - 1, 1, ROWS // 2 - 1)

        def first(I):
            return type(I) is int and I == 0

        def last(I):
            return type(I) is int and I == ROWS - 1

        block = ctx.enter_context(nc.Block())

        @block.sync
        def _(sp):
            sp.dma_start(W_sb[:, :], W).then_inc(small_loaded, 16)
            sp.dma_start(w12[:, 0:1], w1.rearrange("(h o) -> h o", o=1)).then_inc(small_loaded, 16)
            sp.dma_start(w12[:, 1:2], w2.rearrange("(h o) -> h o", o=1)).then_inc(small_loaded, 16)
            sp.dma_start(b_col[:, :], b.rearrange("(h o) -> h o", o=1)).then_inc(small_loaded, 16)
            sp.dma_start(b12[:, 0:1], b1.rearrange("(h o) -> h o", o=1)).then_inc(small_loaded, 16)
            sp.dma_start(b12[:, 1:2], b2.rearrange("(h o) -> h o", o=1)).then_inc(small_loaded, 16)
            for q in range(NC):
                sp.dma_start(in2_stage(q), in2_strips[q]).then_inc(in2_loaded[q % NC], 16)
            for q in range(NC):
                sp.dma_start(x_stage(q), x_strips[q]).then_inc(xs_loaded[q], 16)
            for q in range(NC, NS):
                sp.wait_ge(in2T_ps_ready, HD * (q - NC + 1))
                sp.dma_start(in2_stage(q), in2_strips[q]).then_inc(in2_loaded[q % NC], 16)
            for q in range(NC, NS):
                sp.wait_ge(in2T_ps_ready, HD * (q + 1))
                sp.dma_start(x_stage(q), x_strips[q]).then_inc(xs_loaded[q], 16)

            for c in range(NC):
                sp.wait_ge(hi_ready, c + 1)
                sp.wait_ge(lo_ready, c + 1)
                sp.wait_ge(h_sum_ps_ready, c + 1)
                sp.dma_start(adj_sb[:, c, :], adj_rows[0, :, c, :]).then_inc(adj_loaded[c], 16)
            sp.dma_start(x_res[:, 0, :], x_rows[0]).then_inc(x_loaded[0], 16)

            def body(I, par, half):
                for c in range(NC):
                    if not last(I):
                        sp.wait_ge(p_ready, 4 * I + (c + 1))
                        sp.dma_start(adj_sb[:, c, :], adj_rows[I + 1, :, c, :]).then_inc(adj_loaded[c], 16)
                    if c == 2 and not first(I):
                        sp.wait_ge(o_ready, I)
                        sp.dma_start(out_rows[I - 1], o_sb[:, 1 - par, :]).then_inc(o_stored[1 - par], 16)
                    if c == 2 and not last(I):
                        sp.dma_start(x_res[:, 1 - par, :], x_rows[I + 1]).then_inc(x_loaded[1 - par], 16)

            row_tiles(sp, body)
            sp.wait_ge(o_ready, ROWS)
            sp.dma_start(out_rows[ROWS - 1], o_sb[:, 1, :]).then_inc(o_stored[1], 16)
            for i in range(2):
                sp.wait_ge(o_stored[i], 16 * ROWS // 2)

        @block.gpsimd
        def _(pool):
            nc.gpsimd.memset(ident[:, :], 0.0).then_inc(ident_zero, 1)
            pool.wait_ge(ident_zero, 1)
            nc.gpsimd.affine_select(out=ident[:, :], in_=ident[:, :], compare_op=ALU.not_equal, fill=1.0, base=0,
                                    pattern=[[-1, P]], channel_multiplier=1).then_inc(ident_ready, 1)
            for q in range(NS):
                pool.wait_ge(h_ready, TS * (q + 1))
                pool.wait_ge(hi_ready, q + 1)
                nc.gpsimd.tensor_tensor(H[:, TS * q:TS * (q + 1), 1, 0:D], x_stage(q),
                                        H[:, TS * q:TS * (q + 1), 0, 0:D], ALU.subtract).then_inc(lo_ready, 1)

        @block.scalar
        def _(act):
            for q in range(NS):
                act.wait_ge(in2T_ps_ready, HD * q + 1)
                if q >= 2:
                    act.wait_ge(f_strip_done, q - 1)
                nc.scalar.copy(in2T[:, q % 2, 0, :], tp[:, 0, :]).then_inc(in2T_act, 1)
                act.wait_ge(f2_ps_ready, q + 1)
                nc.scalar.copy(b_all[:, q * STRIP:(q + 1) * STRIP], f2_ps).then_inc(f2_copied, 1)
            act.wait_ge(var_ready, 1)
            nc.scalar.activation(sdev[:, :], sdev[:, :], ACT.Sqrt).then_inc(sdev_ready, 1)
            act.wait_ge(f_max_ready, 1)
            nc.scalar.activation(D_col[:, :], f_col[:, :, 1], ACT.Exp, scale=SLOPE,
                                 bias=tiny[:, 1:2]).then_inc(exps_ready, 1)
            nc.scalar.activation(D_inv[:, :], f_col[:, :, 1], ACT.Exp, scale=-SLOPE,
                                 bias=tiny[:, 2:3]).then_inc(exps_ready, 1)
            nc.scalar.activation(b_all[:, :], b_all[:, :], ACT.Exp, scale=1.0 - SLOPE,
                                 bias=tiny[:, 3:4]).then_inc(exps_ready, 1)
            act.wait_ge(rows_low, 1)
            nc.scalar.activation(g_row[:, :], low[:, 0, :], ACT.Exp).then_inc(exps_ready, 1)
            nc.scalar.activation(c_row[:, :], low[:, 1, :], ACT.Exp).then_inc(exps_ready, 1)
            act.wait_ge(h_affine_ready, 1)
            for j in range(ROWS):
                q, t = divmod(j, TS)
                if t == 0:
                    act.wait_ge(xs_loaded[q], 16)
                nc.scalar.activation(x_stage(q)[:, t, :], x_stage(q)[:, t, :], ACT.Relu, scale=h_mul[:, j:j + 1],
                                     bias=h_add[:, j:j + 1]).then_inc(h_ready, 1)
            act.wait_ge(h_sum_ps_ready, NS)
            nc.scalar.mul(h_sum[:, :], hs_ps, 1.0 / N).then_inc(h_sum_ready, 1)
            act.wait_ge(rows_ready, 1)
            act.wait_ge(hi_ready, NS)
            act.wait_ge(lo_ready, NS)

            def relu_part(I, c):
                nc.scalar.activation(wgt[:, c, :], b_all[:, c * CHUNK:(c + 1) * CHUNK], ACT.Relu,
                                     scale=g_row[:, bass.ds(I, 1)], bias=neg_c[:, bass.ds(I, 1)]).then_inc(r_ready, 1)

            for c in range(NC):
                relu_part(0, c)

            def body(I, par, half):
                for c in range(NC):
                    for k in range(PER * c, PER * c + PER):
                        act.wait_ge(t_ready, 8 * I + (k + 1))
                        nc.scalar.activation(p_hi[:, k % 2, :], tp[:, k % 2, :], ACT.Relu).then_inc(hi_split, 1)
                    if not last(I):
                        relu_part(I + 1, c)

            row_tiles(act, body)

        @block.vector
        def _(dve):
            steps = [0]

            def then_wait(ins):
                steps[0] += 1
                ins.then_inc(dve_step, 1)
                dve.wait_ge(dve_step, steps[0])

            nc.vector.memset(ones[:, :], 1.0).then_inc(ones_ready, 1)
            dve.wait_ge(ones_ready, 1)
            dve.wait_ge(small_loaded, 6 * 16)
            nc.vector.tensor_scalar(b_rep[:, :], ones[:, :], b_col[:, 0:1], None, ALU.mult).then_inc(b_rep_ready, 1)
            dve.wait_ge(u_ps_ready, 1)
            then_wait(nc.vector.tensor_copy(cst[:, :], cst_ps))
            then_wait(nc.vector.tensor_copy(U[:, :, :].rearrange("p h o -> p (h o)"), U_ps))
            for h in range(HD):
                nc.vector.tensor_scalar(U2_rep[:, h, :], ones[:, :], U[:, h, 1:2], None, ALU.mult).then_inc(u_ready, 1)

            def strip_stats(q):
                dve.wait_ge(xs_loaded[q], 16)
                for j in range(TS * q, TS * (q + 1)):
                    ins = nc.vector.bn_stats(out=stats[:, j, :], in_=x_stage(q)[:, j % TS, :])
                then_wait(ins)
                for j in range(TS * q, TS * (q + 1)):
                    ins = nc.vector.bn_aggr(out=mv[:, j, :], in_=stats[:, j, :])
                then_wait(ins)

            for q in range(NS):
                dve.wait_ge(in2T_ps_ready, HD * q + 2)
                if q >= 2:
                    dve.wait_ge(f_strip_done, q - 1)
                nc.vector.tensor_copy(in2T[:, q % 2, 1, :], tp[:, 1, :]).then_inc(in2T_dve, 1)
                dve.wait_ge(f2_copied, q + 1)
                then_wait(nc.vector.reduce_max(f2_max[:, q:q + 1], b_all[:, q * STRIP:(q + 1) * STRIP], AX.X))
                if q < NC:
                    strip_stats(q)
            then_wait(nc.vector.reduce_max(tiny[:, 0:1], f2_max[:, :], AX.X))
            dve.wait_ge(f_strip_done, NS)
            then_wait(nc.vector.tensor_copy(f_col[:, :, :].rearrange("p j o -> p (j o)"), fc_ps))
            then_wait(nc.vector.tensor_scalar(tiny[:, 1:2], tiny[:, 0:1], -SLOPE, None, ALU.mult))
            then_wait(nc.vector.tensor_scalar(tiny[:, 2:3], tiny[:, 0:1], SLOPE, None, ALU.mult))
            nc.vector.tensor_scalar(tiny[:, 3:4], tiny[:, 0:1], SLOPE - 1.0, None, ALU.mult).then_inc(f_max_ready, 1)
            then_wait(nc.vector.tensor_tensor(tiny[:, 4:5], cst[:, 0:1], cst[:, 1:2], ALU.add))
            then_wait(nc.vector.tensor_tensor(tiny[:, 5:6], tiny[:, 4:5], tiny[:, 0:1], ALU.add))
            then_wait(nc.vector.tensor_scalar(t_row[:, :], f_col[:, :, 0], tiny[:, 5:6], 1.0 - SLOPE, ALU.add, ALU.mult))
            then_wait(nc.vector.tensor_scalar(low[:, 0, :], t_row[:, :], 0.0, None, ALU.min))
            nc.vector.tensor_scalar(low[:, 1, :], t_row[:, :], -1.0, 0.0, ALU.mult, ALU.min).then_inc(rows_low, 1)
            for q in range(NC, NS):
                strip_stats(q)
            nc.vector.tensor_scalar(sdev[:, :], mv[:, :, 1], EPS, None, ALU.add).then_inc(var_ready, 1)
            dve.wait_ge(sdev_ready, 1)
            then_wait(nc.vector.reciprocal(rstd[:, :], sdev[:, :]))
            dve.wait_ge(exps_ready, 2)
            then_wait(nc.vector.tensor_scalar(D_big[:, :], D_col[:, :], H_SCALE, None, ALU.mult))
            then_wait(nc.vector.tensor_tensor(h_mul[:, :], rstd[:, :], D_big[:, :], ALU.mult))
            nc.vector.scalar_tensor_tensor(out=h_add[:, :], in0=mv[:, :, 0], scalar=-1.0, in1=h_mul[:, :],
                                           op0=ALU.mult, op1=ALU.mult).then_inc(h_affine_ready, 1)
            then_wait(nc.vector.tensor_scalar(D_inv[:, :], D_inv[:, :], 1.0 / H_SCALE, None, ALU.mult))
            then_wait(nc.vector.tensor_copy(H[:, :, 0, D], D_big[:, :]))
            nc.vector.tensor_tensor(H[:, :, 1, D], D_big[:, :], H[:, :, 0, D], ALU.subtract).then_inc(d_cols_ready, 1)
            dve.wait_ge(exps_ready, 5)
            nc.vector.tensor_scalar(neg_c[:, :], c_row[:, :], -1.0, None, ALU.mult).then_inc(rows_ready, 1)
            for q in range(NS):
                dve.wait_ge(h_ready, TS * (q + 1))
                nc.vector.tensor_copy(H[:, TS * q:TS * (q + 1), 0, 0:D], x_stage(q)).then_inc(hi_ready, 1)
            dve.wait_ge(h_mean_ps_ready, 1)
            nc.vector.tensor_copy(h_mean[:, :], hm_ps).then_inc(h_mean_ready, 1)

            def weights(I, c, whole):
                dve.wait_ge(r_ready, 4 * I + (c + 1))
                dve.wait_ge(adj_loaded[c], 16 * I + 16)
                nc.vector.scalar_tensor_tensor(out=wgt[:, c, :], in0=wgt[:, c, :], scalar=c_row[:, bass.ds(I, 1)],
                                               in1=adj_sb[:, c, :], op0=ALU.add, op1=ALU.min).then_inc(p_ready, 1)

            def finish(I, par, half):
                dve.wait_ge(mm_done, 8 * I + 8)
                nc.vector.tensor_scalar(no_nb[:, par:par + 1], acc[:, par, D:DV], 0.0, None,
                                        ALU.is_equal).then_inc(fin_step, 1)
                dve.wait_ge(fin_step, 4 * I + 1)
                nc.vector.tensor_tensor(den[:, par:par + 1], acc[:, par, D:DV], no_nb[:, par:par + 1],
                                        ALU.add).then_inc(fin_step, 1)
                dve.wait_ge(fin_step, 4 * I + 2)
                nc.vector.reciprocal(r_den[:, par:par + 1], den[:, par:par + 1]).then_inc(fin_step, 1)
                dve.wait_ge(fin_step, 4 * I + 3)
                dve.wait_ge(x_loaded[par], 16 * half + 16)
                nc.vector.scalar_tensor_tensor(out=x_res[:, par, :], in0=acc[:, par, 0:D], scalar=r_den[:, par:par + 1],
                                               in1=x_res[:, par, :], op0=ALU.mult, op1=ALU.add).then_inc(fin_step, 1)
                dve.wait_ge(fin_step, 4 * I + 4)
                dve.wait_ge(o_stored[par], 16 * half)
                nc.vector.scalar_tensor_tensor(out=o_sb[:, par, :], in0=h_mean[:, :], scalar=no_nb[:, par:par + 1],
                                               in1=x_res[:, par, :], op0=ALU.mult, op1=ALU.add).then_inc(o_ready, 1)

            dve.wait_ge(h_mean_ready, 1)
            for c in range(2):
                weights(0, c, 1)

            def body(I, par, half):
                for c in range(NC):
                    if c < 2:
                        weights(I, c + 2, None)
                    elif not last(I):
                        weights(I + 1, c - 2, None)
                    for k in range(PER * c, PER * c + PER):
                        dve.wait_ge(hi_split, 8 * I + (k + 1))
                        nc.vector.scalar_tensor_tensor(out=p_lo[:, k % 2, :], in0=tp[:, k % 2, :], scalar=0.0,
                                                       in1=p_hi[:, k % 2, :], op0=ALU.max,
                                                       op1=ALU.subtract).then_inc(lo_split, 1)
                    if c == 0 and not first(I):
                        finish(I - 1, 1 - par, half - 1 + par)

            row_tiles(dve, body)
            finish(ROWS - 1, 1, ROWS // 2 - 1)

        @block.tensor
        def _(pe):
            pe.wait_ge(small_loaded, 6 * 16)
            pe.wait_ge(b_rep_ready, 1)
            pe.matmul(cst_ps, b_rep[:, :], w12[:, :], start=True, stop=False)
            pe.matmul(cst_ps, ones[0:1, :], b12[:, :], start=False, stop=True)
            for h in range(HD):
                mm = pe.matmul(U_ps[:, 2 * h:2 * h + 2], W_sb[:, h * P:(h + 1) * P], w12[:, :], start=True, stop=True)
            mm.then_inc(u_ps_ready, 1)
            pe.wait_ge(ident_ready, 1)

            def in2_transposes(q):
                pe.wait_ge(in2_loaded[q % NC], 16 * (q // NC + 1))
                for h in range(HD):
                    if q >= 1:
                        pe.wait_ge(in2T_act if h == 0 else in2T_dve, q)
                    for t in range(TS):
                        mm = pe.transpose(tp[:, h, t * P:(t + 1) * P], in2_stage(q)[:, t, h * P:(h + 1) * P],
                                          ident[:, :])
                    mm.then_inc(in2T_ps_ready, 1)

            def f_of_strip(q):
                pe.wait_ge(in2T_act, q + 1)
                pe.wait_ge(in2T_dve, q + 1)
                if q >= 1:
                    pe.wait_ge(f2_copied, q)
                for n in range(STRIP // 512):
                    for h in range(HD):
                        mm = pe.matmul(acc[:, n, :], U2_rep[:, h, :], in2T[:, q % 2, h, n * 512:(n + 1) * 512],
                                       start=(h == 0), stop=(h == HD - 1))
                mm.then_inc(f2_ps_ready, 1)
                for t in range(TS):
                    j = TS * q + t
                    for h in range(HD):
                        mm = pe.matmul(fc_ps[:, 2 * j:2 * j + 2], in2T[:, q % 2, h, t * P:(t + 1) * P], U[:, h, :],
                                       start=(h == 0), stop=(h == HD - 1))
                mm.then_inc(f_strip_done, 1)

            in2_transposes(0)
            pe.wait_ge(u_ready, HD)
            for q in range(NS):
                if q + 1 < NS:
                    in2_transposes(q + 1)
                f_of_strip(q)
            pe.wait_ge(d_cols_ready, 1)
            for j in range(ROWS):
                pe.wait_ge(h_ready, j + 1)
                mm = pe.matmul(hs_ps, D_inv[:, j:j + 1], x_stage(j // TS)[:, j % TS, :],
                               start=(j == 0), stop=(j == ROWS - 1))
                if j % TS == TS - 1:
                    mm.then_inc(h_sum_ps_ready, 1)
            pe.wait_ge(h_sum_ready, 1)
            pe.matmul(hm_ps, ones[0:1, :], h_sum[:, :], start=True, stop=True).then_inc(h_mean_ps_ready, 1)

            def transposes(I, k):
                if k % PER == 0:
                    pe.wait_ge(p_ready, 4 * I + (k // PER + 1))
                for t in range(TS):
                    col = (k % PER) * STRIP + t * P
                    mm = pe.transpose(tp[:, k % 2, t * P:(t + 1) * P], wgt[:, k // PER, col:col + P], ident[:, :])
                mm.then_inc(t_ready, 1)

            def products(I, par, k):
                pe.wait_ge(hi_split, 8 * I + (k + 1))
                for t in range(TS):
                    j = TS * k + t
                    for part in range(2):
                        pe.matmul(acc[:, par, 0:DV], p_hi[:, k % 2, t * P:(t + 1) * P], H[:, j, part, 0:DV],
                                  start=(j == 0 and part == 0), stop=False)
                pe.wait_ge(lo_split, 8 * I + (k + 1))
                for t in range(TS):
                    j = TS * k + t
                    mm = pe.matmul(acc[:, par, 0:DV], p_lo[:, k % 2, t * P:(t + 1) * P], H[:, j, 0, 0:DV],
                                   start=False, stop=(j == ROWS - 1))
                mm.then_inc(mm_done, 1)

            transposes(0, 0)
            transposes(0, 1)

            def body(I, par, half):
                for k in range(NS):
                    if k == 4:
                        pe.wait_ge(o_ready, I)
                    products(I, par, k)
                    if k + 2 < NS:
                        transposes(I, k + 2)
                    elif not last(I):
                        transposes(I + 1, k + 2 - NS)

            row_tiles(pe, body)


_INS = ["x", "adj", "L0_gnn_inlayer2", "L0_gnn_W", "L0_gnn_b", "L0_gnn_w1", "L0_gnn_b1", "L0_gnn_w2", "L0_gnn_b2"]


def kernel(**inputs):
    import numpy as np
    import concourse.bacc as bacc
    from concourse.bass_utils import run_bass_kernel_spmd

    nc = bacc.Bacc("TRN2", target_bir_lowering=False, num_devices=1)
    arrays, args = {}, []
    for name in _INS:
        a = np.ascontiguousarray(inputs[name])
        arrays[f"in_{name}_dram"] = a
        args.append(nc.dram_tensor(f"in_{name}_dram", a.shape, mybir.dt.from_np(a.dtype), kind="ExternalInput").ap())
    out = nc.dram_tensor("out_0_dram", inputs["x"].shape, F32, kind="ExternalOutput").ap()
    graph_attention(nc, *args, out)
    r = run_bass_kernel_spmd(nc, [arrays], core_ids=[0])
    return r.results[0]["out_0_dram"]
```

```python
from contextlib import ExitStack

import concourse.bass as bass
from concourse import mybir

ALU = mybir.AluOpType
ACT = mybir.ActivationFunctionType
AX = mybir.AxisListType
F32 = mybir.dt.float32
F16 = mybir.dt.float16
BF16 = mybir.dt.bfloat16
I32 = mybir.dt.int32

P = 128
B = 32
Q = P // B
SLOPE = 0.01
EPS = 1e-5
H_SCALE = 2.0 ** 11
W_SCALE = 2.0 ** 15


def graph_attention(nc, x, adj, inlayer2, W, b, w1, b1, w2, b2, out):
    N, D = x.shape
    HID = W.shape[0]
    ROWS = N // P
    CHUNK = 4096
    NCH = N // CHUNK
    CQ = CHUNK // Q
    MC = CQ // B
    TS = 8
    NS = ROWS // TS
    SC = MC // TS
    SQ = TS * B
    DV = D + 1
    DVP = D + 2
    HD = D // P
    HALF = TS // 2
    RAW = (TS * 2 * DVP - TS * 2 * D) // 2
    assert HID == P and D == 2 * P and NCH == 2 and SC == Q == 4 and NS == 8

    adj_q = adj.rearrange("(i g r) (c q n) -> i c q r g n", g=Q, r=B, q=Q, n=CQ)
    x_rows = x.rearrange("(i p) d -> i p d", p=P)
    out_rows = out.rearrange("(i p) d -> i p d", p=P)
    x_q = x.rearrange("(c q k t s) d -> c k q s t d", c=NCH, q=Q, k=SC, t=TS)
    in2_q = inlayer2.rearrange("(c q k t s) d -> c k q s t d", c=NCH, q=Q, k=SC, t=TS)

    with ExitStack() as ctx:
        def sb(name, shape, dt):
            return ctx.enter_context(nc.sbuf_tensor(name, shape, dt))

        def sem(name):
            return ctx.enter_context(nc.semaphore(name))

        H = sb("H", [P, ROWS, 2, DVP], F16)
        b_all = sb("b_all", [P, NCH * CQ], F32)
        adj_sb = sb("adj_sb", [P, NCH, Q * CQ], I32)
        mask = sb("mask", [P, NCH, Q * CQ], BF16)
        wgt = sb("wgt", [P, NCH, Q, CQ], F32)
        wT = sb("wT", [P, 4, TS, P], F32)
        w_lo = sb("w_lo", [P, 4, TS, P], F16)
        gc = sb("gc", [P, 2, Q * ROWS], F32)
        neg_c = sb("neg_c", [P, Q * ROWS], F32)
        x_res = sb("x_res", [P, 2, D], F32)
        o_sb = sb("o_sb", [P, 2, D], F32)
        h_mean = sb("h_mean", [P, D], F32)
        no_nb = sb("no_nb", [P, 2], F32)
        den = sb("den", [P, 2], F32)
        r_den = sb("r_den", [P, 2], F32)
        h_f32 = sb("h_f32", [P, 2, HALF, D], F32)
        ident = sb("ident", [P, P], F32)
        quads = sb("quads", [P, P], F32)
        pick = sb("pick", [P, Q, P], F32)
        same = sb("same", [P, B], F32)
        W_sb = sb("W_sb", [P, D], F32)
        w12 = sb("w12", [P, 2], F32)
        b_col = sb("b_col", [P, 1], F32)
        b12 = sb("b12", [1, 2], F32)
        ones = sb("ones", [P, P], F32)
        b_rep = sb("b_rep", [P, P], F32)
        U = sb("U", [P, HD, 2], F32)
        cst = sb("cst", [P, 2], F32)
        f_col = sb("f_col", [P, ROWS, 2], F32)
        stats = sb("stats", [P, ROWS, 6], F32)
        mv = sb("mv", [P, ROWS, 2], F32)
        tiny = sb("tiny", [P, 8], F32)
        f2_rel = sb("f2_rel", [P, ROWS], F32)
        t_row = sb("t_row", [P, ROWS], F32)
        low = sb("low", [P, 2, ROWS], F32)
        minus_half = sb("minus_half", [P, TS], F32)
        var_eps = sb("var_eps", [P, ROWS], F32)
        rstd = sb("rstd", [P, ROWS], F32)
        D_big = sb("D_big", [P, ROWS], F32)
        D_inv = sb("D_inv", [P, ROWS], F32)
        D_parts = sb("D_parts", [P, ROWS, 2], F16)
        D_inv_parts = sb("D_inv_parts", [P, ROWS, 2], F16)
        h_mul = sb("h_mul", [P, ROWS], F32)
        h_add = sb("h_add", [P, ROWS], F32)
        h_sum = sb("h_sum", [2, D], F32)

        rp = ctx.enter_context(nc.psum_tensor("rp", [P, 2, CQ], F32))
        acc = ctx.enter_context(nc.psum_tensor("acc", [P, 2, 512], F32))
        small = ctx.enter_context(nc.psum_tensor("small", [P, 2, 512], F32))
        t_ps = small[:, 0, :]
        hm_ps = small[:, 0, 0:D]
        fc_ps = small[:, 1, 0:2 * ROWS]
        cst_ps = small[:, 1, 2 * ROWS:2 * ROWS + 2]
        U_ps = small[:, 1, 2 * ROWS + 2:2 * ROWS + 2 + 2 * HD]
        fm_ps = small[0:1, 1, 256:256 + P]
        F_ps = small[:, 1, 384:385]
        hs_ps = small[0:2, 1, 0:D]
        b_ps = rp[:, :, :].rearrange("p a n -> p (a n)")

        w_hi = wT[:, :, :, :].rearrange("p a t i -> p (a t i)").bitcast(BF16).rearrange(
            "p (a t i e) -> p a t i e", a=4, t=TS, e=2)[:, :, :, :, 1]

        def in2_stage(k):
            slot = wgt[:, k // 2, :, :].rearrange("p g n -> p (g n)") if k < 4 else \
                adj_sb[:, (k - 4) // 2, :].bitcast(F32)
            return slot[:, (k % 2) * TS * D:(k % 2 + 1) * TS * D].rearrange("p (t d) -> p t d", d=D)

        def x_stage(k):
            room = H[:, TS * k:TS * (k + 1), :, :].rearrange("p t a d -> p (t a d)").bitcast(F32)
            return room[:, RAW:RAW + TS * D].rearrange("p (t d) -> p t d", d=D)

        in2T = wT[:, :, :, :].rearrange("p (a h) t i -> p a h (t i)", h=HD)
        f2_blocks = w_lo[:, :, :, :].rearrange("p a t i -> p (a t i)").bitcast(F32).rearrange(
            "p (j s) -> p j s", s=B)

        small_loaded = sem("small_loaded")
        in2_loaded = [sem(f"in2_loaded{i}") for i in range(NS)]
        xs_loaded = [sem(f"xs_loaded{i}") for i in range(NS)]
        zeroed = sem("zeroed")
        ident_ready = sem("ident_ready")
        quads_ready = sem("quads_ready")
        ones_ready = sem("ones_ready")
        b_rep_ready = sem("b_rep_ready")
        pick_ready = sem("pick_ready")
        u_ps_ready = sem("u_ps_ready")
        u_ready = sem("u_ready")
        in2T_ps_ready = sem("in2T_ps_ready")
        in2T_act = sem("in2T_act")
        in2T_dve = sem("in2T_dve")
        f_strip_done = sem("f_strip_done")
        dve_step = sem("dve_step")
        f_max_part = sem("f_max_part")
        fm_ps_ready = sem("fm_ps_ready")
        f_max_ready = sem("f_max_ready")
        F_ps_ready = sem("F_ps_ready")
        f2_rel_ready = sem("f2_rel_ready")
        blocks_ready = sem("blocks_ready")
        b_ps_ready = sem("b_ps_ready")
        b_ready = sem("b_ready")
        low_ready = sem("low_ready")
        t_ps_ready = sem("t_ps_ready")
        gc_exp = sem("gc_exp")
        gc_ready = sem("gc_ready")
        D_exp = sem("D_exp")
        d_parts_ready = sem("d_parts_ready")
        var_ready = sem("var_ready")
        rstd_ready = sem("rstd_ready")
        h_affine_ready = sem("h_affine_ready")
        h_ready = sem("h_ready")
        hi_ready = sem("hi_ready")
        lo_ready = sem("lo_ready")
        h_sum_done = sem("h_sum_done")
        h_sum_ready = sem("h_sum_ready")
        h_mean_ps_ready = sem("h_mean_ps_ready")
        h_mean_ready = sem("h_mean_ready")
        adj_loaded = [sem(f"adj_loaded{c}") for c in range(NCH)]
        m_ready = sem("m_ready")
        r_ready = sem("r_ready")
        p_ready = sem("p_ready")
        t_ready = sem("t_ready")
        lo_split = sem("lo_split")
        mm_done = sem("mm_done")
        x_loaded = [sem(f"x_loaded{i}") for i in range(2)]
        fin_step = sem("fin_step")
        o_ready = sem("o_ready")
        o_stored = [sem(f"o_stored{i}") for i in range(2)]

        def row_tiles(eng, body):
            body(0, 0, 0)
            with eng.Fori(0, ROWS // 2 - 1) as v:
                body(2 * v + 1, 1, v)
                body(2 * v + 2, 0, v + 1)
            body(ROWS - 1, 1, ROWS // 2 - 1)

        def is_row(I, n):
            return type(I) is int and I == n

        block = ctx.enter_context(nc.Block())

        def load_strip(eng, stage, source, k, signal, quadrants):
            for q in quadrants:
                eng.dma_start(stage[B * q:B * (q + 1), :, :], source[k // SC, k % SC, q]).then_inc(signal, 16)

        def load_adj(eng, I, c, quadrants):
            for q in quadrants:
                eng.dma_start(adj_sb[B * q:B * (q + 1), c, :].rearrange("p (g n) -> p g n", g=Q),
                              adj_q[I, c, q]).then_inc(adj_loaded[c], 16)

        def first_loads(eng, quadrants):
            for k in range(NS):
                load_strip(eng, in2_stage(k), in2_q, k, in2_loaded[k], quadrants)
            for k in range(2):
                load_strip(eng, x_stage(k), x_q, k, xs_loaded[k], quadrants)

        def second_loads(eng, quadrants):
            eng.wait_ge(in2T_ps_ready, HD * 6)
            load_adj(eng, 0, 0, quadrants)
            for k in range(2, 5):
                load_strip(eng, x_stage(k), x_q, k, xs_loaded[k], quadrants)

        def third_loads(eng, quadrants):
            eng.wait_ge(in2T_ps_ready, HD * 8)
            load_adj(eng, 0, 1, quadrants)
            for k in range(5, NS):
                load_strip(eng, x_stage(k), x_q, k, xs_loaded[k], quadrants)

        @block.sync
        def _(sp):
            sp.dma_start(W_sb[:, :], W).then_inc(small_loaded, 16)
            sp.dma_start(w12[:, 0:1], w1.rearrange("(h o) -> h o", o=1)).then_inc(small_loaded, 16)
            sp.dma_start(w12[:, 1:2], w2.rearrange("(h o) -> h o", o=1)).then_inc(small_loaded, 16)
            sp.dma_start(b_col[:, :], b.rearrange("(h o) -> h o", o=1)).then_inc(small_loaded, 16)
            sp.dma_start(b12[:, 0:1], b1.rearrange("(h o) -> h o", o=1)).then_inc(small_loaded, 16)
            sp.dma_start(b12[:, 1:2], b2.rearrange("(h o) -> h o", o=1)).then_inc(small_loaded, 16)
            first_loads(sp, (0, 1))
            second_loads(sp, (0, 1))
            third_loads(sp, (0, 1))
            sp.dma_start(x_res[:, 0, :], x_rows[0]).then_inc(x_loaded[0], 16)

            def body(I, par, half):
                if not is_row(I, ROWS - 1):
                    for c in range(NCH):
                        sp.wait_ge(m_ready, 8 * I + Q * (c + 1))
                        load_adj(sp, I + 1, c, (0, 1))
                if not is_row(I, 0):
                    sp.wait_ge(o_ready, I)
                    sp.dma_start(out_rows[I - 1], o_sb[:, 1 - par, :]).then_inc(o_stored[1 - par], 16)
                if not is_row(I, ROWS - 1):
                    sp.dma_start(x_res[:, 1 - par, :], x_rows[I + 1]).then_inc(x_loaded[1 - par], 16)

            row_tiles(sp, body)
            sp.wait_ge(o_ready, ROWS)
            sp.dma_start(out_rows[ROWS - 1], o_sb[:, 1, :]).then_inc(o_stored[1], 16)
            for i in range(2):
                sp.wait_ge(o_stored[i], 16 * ROWS // 2)

        @block.gpsimd
        def _(pool):
            nc.gpsimd.memset(ident[:, :], 0.0).then_inc(zeroed, 1)
            nc.gpsimd.memset(minus_half[:, :], -0.5).then_inc(zeroed, 1)
            pool.wait_ge(zeroed, 2)
            nc.gpsimd.affine_select(out=ident[:, :], in_=ident[:, :], compare_op=ALU.not_equal, fill=1.0, base=0,
                                    pattern=[[-1, P]], channel_multiplier=1).then_inc(ident_ready, 1)

            def rstds(k):
                pool.wait_ge(var_ready, k + 1)
                nc.gpsimd.tensor_tensor(rstd[:, TS * k:TS * (k + 1)], var_eps[:, TS * k:TS * (k + 1)],
                                        minus_half[:, :], ALU.pow).then_inc(rstd_ready, 1)

            def low_of_values(n):
                pool.wait_ge(h_ready, HALF * (n + 1))
                pool.wait_ge(hi_ready, n + 1)
                nc.gpsimd.tensor_tensor(H[:, HALF * n:HALF * (n + 1), 1, 0:D], h_f32[:, n % 2, :, :],
                                        H[:, HALF * n:HALF * (n + 1), 0, 0:D], ALU.subtract).then_inc(lo_ready, 1)

            def low_of_weights(I, k):
                pool.wait_ge(t_ready, 8 * I + (k + 1))
                nc.gpsimd.tensor_tensor(w_lo[:, k % 4, :, :], wT[:, k % 4, :, :], w_hi[:, k % 4, :, :],
                                        ALU.subtract).then_inc(lo_split, 1)

            rstds(0)
            for k in range(NS):
                if k + 1 < NS:
                    rstds(k + 1)
                low_of_values(2 * k)
                low_of_values(2 * k + 1)
                if k >= 1:
                    low_of_weights(0, k - 1)
            low_of_weights(0, NS - 1)
            with pool.Fori(1, ROWS) as I:
                for k in range(NS):
                    low_of_weights(I, k)

        @block.scalar
        def _(act):
            first_loads(act, (2, 3))
            for k in range(NS):
                act.wait_ge(in2T_ps_ready, HD * k + 1)
                if k >= 2:
                    act.wait_ge(f_strip_done, k - 1)
                nc.scalar.copy(in2T[:, k % 2, 0, :], rp[:, 0, :]).then_inc(in2T_act, 1)
                if k == 6:
                    second_loads(act, (2, 3))
            third_loads(act, (2, 3))
            act.wait_ge(f2_rel_ready, 1)
            nc.scalar.activation(D_big[:, :], f2_rel[:, :], ACT.Exp, scale=SLOPE).then_inc(D_exp, 1)
            nc.scalar.activation(D_inv[:, :], f2_rel[:, :], ACT.Exp, scale=-SLOPE).then_inc(D_exp, 1)
            act.wait_ge(t_ps_ready, 1)
            for kind in range(2):
                nc.scalar.activation(gc[:, kind, :].rearrange("p (c q m) -> p q c m", c=NCH, q=Q),
                                     t_ps.rearrange("p (q e c m) -> p q e c m", q=Q, e=2, c=NCH)[:, :, kind, :, :],
                                     ACT.Exp).then_inc(gc_exp, 1)
            act.wait_ge(b_ps_ready, 1)
            nc.scalar.activation(b_all[:, :], b_ps, ACT.Exp, scale=1.0 - SLOPE).then_inc(b_ready, 1)

            def relu_part(I, g, c):
                nc.scalar.activation(rp[:, g % 2, :], b_all[:, c * CQ:(c + 1) * CQ], ACT.Relu,
                                     scale=gc[:, 0, bass.ds(Q * I + g, 1)],
                                     bias=neg_c[:, bass.ds(Q * I + g, 1)]).then_inc(r_ready, 1)

            def mask_part(I, g, c):
                if g == 0:
                    act.wait_ge(adj_loaded[c], 64 * I + 64)
                nc.scalar.activation(mask[:, c, g * CQ:(g + 1) * CQ], adj_sb[:, c, g * CQ:(g + 1) * CQ], ACT.Relu,
                                     scale=W_SCALE).then_inc(m_ready, 1)

            def values(k):
                act.wait_ge(h_affine_ready, k + 1)
                for j in range(TS * k, TS * (k + 1)):
                    n = j // HALF
                    if j % HALF == 0 and n >= 2:
                        act.wait_ge(hi_ready, n - 1)
                        act.wait_ge(lo_ready, n - 1)
                    nc.scalar.activation(h_f32[:, n % 2, j % HALF, :], x_stage(k)[:, j % TS, :], ACT.Relu,
                                         scale=h_mul[:, j:j + 1], bias=h_add[:, j:j + 1]).then_inc(h_ready, 1)

            for g in range(Q):
                mask_part(0, g, 0)
            act.wait_ge(gc_ready, 1)
            act.wait_ge(b_ready, 1)
            relu_part(0, 0, 0)
            relu_part(0, 1, 0)
            for n in range(2, 5):
                if n == 2:
                    values(0)
                act.wait_ge(p_ready, n - 1)
                relu_part(0, n % Q, n // Q)
            act.wait_ge(m_ready, Q)
            load_adj(act, 1, 0, (2, 3))
            for g in range(Q):
                mask_part(0, g, 1)
            act.wait_ge(m_ready, 2 * Q)
            load_adj(act, 1, 1, (2, 3))

            def body(I):
                for u in range(NS):
                    c, g = divmod(u, Q)
                    if is_row(I, 0) and u + 1 < NS:
                        values(u + 1)
                    if g == 3 and not is_row(I, ROWS - 1):
                        mask_part(I + 1, g, c)
                    n = u + 5
                    if n < 2 * Q:
                        act.wait_ge(p_ready, 8 * I + (n - 1))
                        act.nop(nofuse=True)
                        relu_part(I, n % Q, n // Q)
                    elif not is_row(I, ROWS - 1):
                        act.wait_ge(p_ready, 8 * I + (n - 1))
                        act.nop(nofuse=True)
                        relu_part(I + 1, n % Q, n // Q - NCH)
                    if g < 3 and not is_row(I, ROWS - 1):
                        mask_part(I + 1, g, c)
                    if g == 3 and not (is_row(I, ROWS - 1) or is_row(I, ROWS - 2)):
                        act.wait_ge(m_ready, 8 * I + (8 + Q * (c + 1)))
                        load_adj(act, I + 2, c, (2, 3))

            body(0)
            with act.Fori(1, ROWS - 2) as I:
                body(I)
            body(ROWS - 2)
            body(ROWS - 1)

        @block.vector
        def _(dve):
            steps = [0]

            def then_wait(ins):
                steps[0] += 1
                ins.then_inc(dve_step, 1)
                dve.wait_ge(dve_step, steps[0])

            nc.vector.memset(ones[:, :], 1.0).then_inc(ones_ready, 1)
            then_wait(nc.vector.memset(quads[:, :], 0.0))
            for q in range(Q):
                nc.vector.memset(quads[B * q:B * (q + 1), B * q:B * (q + 1)], 1.0).then_inc(quads_ready, 1)
            dve.wait_ge(ones_ready, 1)
            dve.wait_ge(small_loaded, 6 * 16)
            nc.vector.tensor_scalar(b_rep[:, :], ones[:, :], b_col[:, 0:1], None, ALU.mult).then_inc(b_rep_ready, 1)
            dve.wait_ge(ident_ready, 1)
            for q in range(Q):
                nc.vector.tensor_copy(pick[:, q, :].rearrange("p (a r) -> p a r", a=Q),
                                      ident[:, B * q:B * (q + 1)].unsqueeze(1).broadcast_to([P, Q, B])
                                      ).then_inc(pick_ready, 1)
            nc.vector.tensor_reduce(same[:, :], ident[:, :].rearrange("p (q s) -> p s q", q=Q), AX.X,
                                    ALU.add).then_inc(pick_ready, 1)
            dve.wait_ge(u_ps_ready, 1)
            nc.vector.tensor_copy(cst[:, :], cst_ps).then_inc(u_ready, 1)
            nc.vector.tensor_copy(U[:, :, :].rearrange("p h o -> p (h o)"), U_ps).then_inc(u_ready, 1)
            for k in range(NS):
                dve.wait_ge(in2T_ps_ready, HD * k + 2)
                if k >= 2:
                    dve.wait_ge(f_strip_done, k - 1)
                nc.vector.tensor_copy(in2T[:, k % 2, 1, :], rp[:, 1, :]).then_inc(in2T_dve, 1)

            def strip_stats(k):
                dve.wait_ge(xs_loaded[k], 64)
                for j in range(TS * k, TS * (k + 1)):
                    ins = nc.vector.bn_stats(out=stats[:, j, :], in_=x_stage(k)[:, j % TS, :])
                then_wait(ins)
                for j in range(TS * k, TS * (k + 1)):
                    ins = nc.vector.bn_aggr(out=mv[:, j, :], in_=stats[:, j, :])
                then_wait(ins)
                nc.vector.tensor_scalar(var_eps[:, TS * k:TS * (k + 1)], mv[:, TS * k:TS * (k + 1), 1], EPS, None,
                                        ALU.add).then_inc(var_ready, 1)

            dve.wait_ge(u_ready, 2)
            dve.wait_ge(f_strip_done, NS)
            then_wait(nc.vector.tensor_copy(f_col[:, :, :].rearrange("p j o -> p (j o)"), fc_ps))
            nc.vector.reduce_max(tiny[:, 0:1], f_col[:, :, 1], AX.X).then_inc(f_max_part, 1)
            dve.wait_ge(fm_ps_ready, 1)
            nc.vector.reduce_max(tiny[0:1, 1:2], fm_ps, AX.X).then_inc(f_max_ready, 1)
            then_wait(nc.vector.tensor_tensor(tiny[:, 4:5], cst[:, 0:1], cst[:, 1:2], ALU.add))
            dve.wait_ge(F_ps_ready, 1)
            then_wait(nc.vector.tensor_copy(tiny[:, 2:3], F_ps))
            nc.vector.tensor_scalar(f2_rel[:, :], f_col[:, :, 1], tiny[:, 2:3], None,
                                    ALU.subtract).then_inc(f2_rel_ready, 1)
            then_wait(nc.vector.tensor_tensor(tiny[:, 5:6], tiny[:, 4:5], tiny[:, 2:3], ALU.add))
            then_wait(nc.vector.tensor_scalar(t_row[:, :], f_col[:, :, 0], tiny[:, 5:6], 1.0 - SLOPE, ALU.add, ALU.mult))
            nc.vector.tensor_scalar(low[:, 0, :], t_row[:, :], 0.0, None, ALU.min).then_inc(low_ready, 1)
            nc.vector.tensor_scalar(low[:, 1, :], t_row[:, :], -1.0, 0.0, ALU.mult, ALU.min).then_inc(low_ready, 1)
            dve.wait_ge(f2_rel_ready, 1)
            dve.wait_ge(pick_ready, Q + 1)
            nc.vector.tensor_tensor(f2_blocks, f2_rel[:, :].unsqueeze(2).broadcast_to([P, ROWS, B]),
                                    same[:, :].unsqueeze(1).broadcast_to([P, ROWS, B]),
                                    ALU.mult).then_inc(blocks_ready, 1)
            dve.wait_ge(gc_exp, 2)
            then_wait(nc.vector.tensor_scalar(gc[:, :, :], gc[:, :, :], W_SCALE, None, ALU.mult))
            nc.vector.tensor_scalar(neg_c[:, :], gc[:, 1, :], -1.0, None, ALU.mult).then_inc(gc_ready, 1)
            dve.wait_ge(D_exp, 2)
            then_wait(nc.vector.tensor_scalar(D_big[:, :], D_big[:, :], H_SCALE, None, ALU.mult))
            nc.vector.tensor_copy(D_parts[:, :, 0], D_big[:, :])
            then_wait(nc.vector.tensor_copy(D_inv_parts[:, :, 0], D_inv[:, :]))
            nc.vector.tensor_tensor(D_parts[:, :, 1], D_big[:, :], D_parts[:, :, 0], ALU.subtract)
            then_wait(nc.vector.tensor_tensor(D_inv_parts[:, :, 1], D_inv[:, :], D_inv_parts[:, :, 0], ALU.subtract))

            def affine(k):
                at = slice(TS * k, TS * (k + 1))
                dve.wait_ge(rstd_ready, k + 1)
                then_wait(nc.vector.tensor_tensor(h_mul[:, at], rstd[:, at], D_big[:, at], ALU.mult))
                nc.vector.scalar_tensor_tensor(out=h_add[:, at], in0=mv[:, at, 0], scalar=-1.0, in1=h_mul[:, at],
                                               op0=ALU.mult, op1=ALU.mult).then_inc(h_affine_ready, 1)

            def high_of_values(n):
                at = slice(HALF * n, HALF * (n + 1))
                dve.wait_ge(h_ready, HALF * (n + 1))
                nc.vector.tensor_copy(H[:, at, :, D], D_parts[:, at, :])
                nc.vector.tensor_copy(H[:, at, 0, 0:D], h_f32[:, n % 2, :, :]).then_inc(hi_ready, 1)

            def weights(I, g, c):
                dve.wait_ge(r_ready, 8 * I + (Q * c + g + 1))
                dve.wait_ge(m_ready, 8 * I + (Q * c + g + 1))
                nc.vector.scalar_tensor_tensor(out=wgt[:, c, g, :], in0=rp[:, g % 2, :],
                                               scalar=gc[:, 1, bass.ds(Q * I + g, 1)],
                                               in1=mask[:, c, g * CQ:(g + 1) * CQ], op0=ALU.add,
                                               op1=ALU.min).then_inc(p_ready, 1)

            def turn(I, k):
                c, s = divmod(k, SC)
                dve.wait_ge(p_ready, 8 * I + Q * (c + 1))
                if not (is_row(I, 0) and k < 4):
                    dve.wait_ge(mm_done, 8 * I + (k - 3) if k >= 3 else 8 * I - (3 - k))
                nc.vector.transpose(wT[:, k % 4, :, :].rearrange("p t (g r) -> p g t r", g=Q),
                                    wgt[:, c, :, s * SQ:(s + 1) * SQ]).then_inc(t_ready, 1)

            def finish_0(I, par, half):
                dve.wait_ge(mm_done, 8 * I + 8)
                nc.vector.tensor_scalar(no_nb[:, par:par + 1], acc[:, par, D:DV], 0.0, None,
                                        ALU.is_equal).then_inc(fin_step, 1)

            def finish_1(I, par, half):
                dve.wait_ge(fin_step, 4 * I + 1)
                nc.vector.tensor_tensor(den[:, par:par + 1], acc[:, par, D:DV], no_nb[:, par:par + 1],
                                        ALU.add).then_inc(fin_step, 1)

            def finish_2(I, par, half):
                dve.wait_ge(fin_step, 4 * I + 2)
                nc.vector.reciprocal(r_den[:, par:par + 1], den[:, par:par + 1]).then_inc(fin_step, 1)

            def finish_3(I, par, half):
                dve.wait_ge(fin_step, 4 * I + 3)
                dve.wait_ge(x_loaded[par], 16 * half + 16)
                nc.vector.scalar_tensor_tensor(out=x_res[:, par, :], in0=acc[:, par, 0:D], scalar=r_den[:, par:par + 1],
                                               in1=x_res[:, par, :], op0=ALU.mult, op1=ALU.add).then_inc(fin_step, 1)

            def finish_4(I, par, half):
                dve.wait_ge(fin_step, 4 * I + 4)
                dve.wait_ge(o_stored[par], 16 * half)
                nc.vector.scalar_tensor_tensor(out=o_sb[:, par, :], in0=h_mean[:, :], scalar=no_nb[:, par:par + 1],
                                               in1=x_res[:, par, :], op0=ALU.mult, op1=ALU.add).then_inc(o_ready, 1)

            strip_stats(0)
            affine(0)
            weights(0, 0, 0)
            weights(0, 1, 0)
            strip_stats(1)
            high_of_values(0)
            high_of_values(1)
            affine(1)
            weights(0, 2, 0)
            weights(0, 3, 0)

            def body(I, par, half):
                def finish_previous(step):
                    if not is_row(I, 0):
                        step(I - 1, 1 - par, half - 1 + par)

                def next_weights(g, c):
                    if c == 0:
                        weights(I, g, 1)
                    elif not is_row(I, ROWS - 1):
                        weights(I + 1, g, 0)

                for u in range(NS):
                    c, g = divmod(u, Q)
                    if g == 0:
                        turn(I, u)
                        if not is_row(I, 0) or c == 1:
                            dve.wait_ge(t_ready, 8 * I + u)
                        if u == 4:
                            finish_previous(finish_1)
                        next_weights(g, c)
                        if u == 4:
                            finish_previous(finish_2)
                    else:
                        next_weights(g, c)
                        if u == 5:
                            finish_previous(finish_3)
                        turn(I, u)
                        if u == 3:
                            finish_previous(finish_0)
                        if u == 5:
                            finish_previous(finish_4)
                    if is_row(I, 0):
                        if u + 2 < NS:
                            strip_stats(u + 2)
                        if u + 1 < NS:
                            high_of_values(2 * u + 2)
                            high_of_values(2 * u + 3)
                        if u + 2 < NS:
                            affine(u + 2)
                if is_row(I, 0):
                    dve.wait_ge(h_sum_done, 1)
                    nc.vector.tensor_scalar(h_sum[:, :], hs_ps, 1.0 / (H_SCALE * N), None,
                                            ALU.mult).then_inc(h_sum_ready, 1)
                    dve.wait_ge(h_mean_ps_ready, 1)
                    then_wait(nc.vector.tensor_copy(h_mean[:, :], hm_ps))

            row_tiles(dve, body)
            for step in (finish_0, finish_1, finish_2, finish_3, finish_4):
                step(ROWS - 1, 1, ROWS // 2 - 1)

        @block.tensor
        def _(pe):
            pe.wait_ge(small_loaded, 6 * 16)
            pe.wait_ge(b_rep_ready, 1)
            pe.matmul(cst_ps, b_rep[:, :], w12[:, :], start=True, stop=False)
            pe.matmul(cst_ps, ones[0:1, :], b12[:, :], start=False, stop=True)
            for h in range(HD):
                mm = pe.matmul(U_ps[:, 2 * h:2 * h + 2], W_sb[:, h * P:(h + 1) * P], w12[:, :], start=True, stop=True)
            mm.then_inc(u_ps_ready, 1)
            pe.wait_ge(ident_ready, 1)

            def in2_transposes(k):
                pe.wait_ge(in2_loaded[k], 64)
                for h in range(HD):
                    if k >= 1:
                        pe.wait_ge(in2T_act if h == 0 else in2T_dve, k)
                    for t in range(TS):
                        mm = pe.transpose(rp[:, h, t * P:(t + 1) * P], in2_stage(k)[:, t, h * P:(h + 1) * P],
                                          ident[:, :])
                    mm.then_inc(in2T_ps_ready, 1)

            def f_of_strip(k):
                pe.wait_ge(in2T_act, k + 1)
                pe.wait_ge(in2T_dve, k + 1)
                for t in range(TS):
                    j = TS * k + t
                    for h in range(HD):
                        mm = pe.matmul(fc_ps[:, 2 * j:2 * j + 2], in2T[:, k % 2, h, t * P:(t + 1) * P], U[:, h, :],
                                       start=(h == 0), stop=(h == HD - 1))
                mm.then_inc(f_strip_done, 1)

            in2_transposes(0)
            pe.wait_ge(u_ready, 2)
            for k in range(NS):
                if k + 1 < NS:
                    in2_transposes(k + 1)
                f_of_strip(k)
            pe.wait_ge(f_max_part, 1)
            pe.transpose(fm_ps, tiny[:, 0:1], ident[:, :]).then_inc(fm_ps_ready, 1)
            pe.wait_ge(f_max_ready, 1)
            pe.matmul(F_ps, ones[0:1, :], tiny[0:1, 1:2], start=True, stop=True).then_inc(F_ps_ready, 1)
            pe.wait_ge(low_ready, 2)
            pe.wait_ge(pick_ready, Q + 1)
            for q in range(Q):
                mm = pe.matmul(t_ps[:, 2 * ROWS * q:2 * ROWS * (q + 1)], pick[:, q, :],
                               low[:, :, :].rearrange("p e j -> p (e j)"), start=True, stop=True)
            mm.then_inc(t_ps_ready, 1)
            pe.wait_ge(blocks_ready, 1)
            pe.wait_ge(quads_ready, Q)
            for n in range(4):
                mm = pe.matmul(b_ps[:, n * 512:(n + 1) * 512], quads[:, :],
                               f2_blocks[:, n * 16:(n + 1) * 16, :].rearrange("p j s -> p (j s)"),
                               start=True, stop=True)
            mm.then_inc(b_ps_ready, 1)

            def products(I, par, k):
                pe.wait_ge(t_ready, 8 * I + (k + 1))
                for t in range(TS):
                    j = TS * k + t
                    for part in range(2):
                        pe.matmul(acc[:, par, 0:DV], w_hi[:, k % 4, t, :], H[:, j, part, 0:DV],
                                  start=(j == 0 and part == 0), stop=False)
                pe.wait_ge(lo_split, 8 * I + (k + 1))
                for t in range(TS):
                    j = TS * k + t
                    mm = pe.matmul(acc[:, par, 0:DV], w_lo[:, k % 4, t, :], H[:, j, 0, 0:DV],
                                   start=False, stop=(j == ROWS - 1))
                mm.then_inc(mm_done, 1)

            def sum_of_values(k):
                for j in range(TS * k, TS * (k + 1)):
                    for part in range(2):
                        mm = pe.matmul(hs_ps, D_inv_parts[:, j, :], H[:, j, part, 0:D],
                                       start=(j == 0 and part == 0), stop=(j == ROWS - 1 and part == 1))
                return mm

            def body(I, par, half):
                for k in range(NS):
                    if k == NS - 1:
                        pe.wait_ge(o_ready, I)
                    if is_row(I, 0):
                        pe.wait_ge(hi_ready, 2 * k + 2)
                        pe.wait_ge(lo_ready, 2 * k + 2)
                    products(I, par, k)
                    if is_row(I, 0):
                        mm = sum_of_values(k)
                if is_row(I, 0):
                    mm.then_inc(h_sum_done, 1)
                    pe.wait_ge(h_sum_ready, 1)
                    pe.matmul(hm_ps, ones[0:2, :], h_sum[:, :], start=True, stop=True).then_inc(h_mean_ps_ready, 1)

            row_tiles(pe, body)


_INS = ["x", "adj", "L0_gnn_inlayer2", "L0_gnn_W", "L0_gnn_b", "L0_gnn_w1", "L0_gnn_b1", "L0_gnn_w2", "L0_gnn_b2"]


def kernel(**inputs):
    import numpy as np
    import concourse.bacc as bacc
    from concourse.bass_utils import run_bass_kernel_spmd

    nc = bacc.Bacc("TRN2", target_bir_lowering=False, num_devices=1)
    arrays, args = {}, []
    for name in _INS:
        a = np.ascontiguousarray(inputs[name])
        arrays[f"in_{name}_dram"] = a
        args.append(nc.dram_tensor(f"in_{name}_dram", a.shape, mybir.dt.from_np(a.dtype), kind="ExternalInput").ap())
    out = nc.dram_tensor("out_0_dram", inputs["x"].shape, F32, kind="ExternalOutput").ap()
    graph_attention(nc, *args, out)
    r = run_bass_kernel_spmd(nc, [arrays], core_ids=[0])
    return r.results[0]["out_0_dram"]
```

```python
from contextlib import ExitStack

import concourse.bass as bass
from concourse import mybir

ALU = mybir.AluOpType
ACT = mybir.ActivationFunctionType
AX = mybir.AxisListType
F32 = mybir.dt.float32
F16 = mybir.dt.float16
BF16 = mybir.dt.bfloat16
I32 = mybir.dt.int32

P = 128
B = 32
Q = P // B
SLOPE = 0.01
EPS = 1e-5
H_SCALE = 2.0 ** 11
W_SCALE = 2.0 ** 15


def graph_attention(nc, x, adj, inlayer2, W, b, w1, b1, w2, b2, out):
    N, D = x.shape
    HID = W.shape[0]
    ROWS = N // P
    CHUNK = 4096
    NCH = N // CHUNK
    CQ = CHUNK // Q
    MC = CQ // B
    TS = 8
    NS = ROWS // TS
    SC = MC // TS
    SQ = TS * B
    DV = D + 1
    DVP = D + 2
    HALF = TS // 2
    HR = 3
    RAW = (TS * 2 * DVP - TS * 2 * D) // 2
    FM = D // B
    assert HID == P and HALF == Q and D == 2 * P and NCH == 2 and SC == Q == 4 and NS == 8

    adj_q = adj.rearrange("(i g r) (c q n) -> i g c q r n", g=Q, r=B, q=Q, n=CQ)
    x_rows = x.rearrange("(i p) d -> i p d", p=P)
    out_rows = out.rearrange("(i p) d -> i p d", p=P)
    x_q = x.rearrange("(c q k t s) d -> c k q s t d", c=NCH, q=Q, k=SC, t=TS)
    in2_q = inlayer2.rearrange("(c q k t s) d -> c k q s t d", c=NCH, q=Q, k=SC, t=TS)

    with ExitStack() as ctx:
        def sb(name, shape, dt):
            return ctx.enter_context(nc.sbuf_tensor(name, shape, dt))

        def sem(name):
            return ctx.enter_context(nc.semaphore(name))

        H = sb("H", [P, ROWS, 2, DVP], F16)
        b_all = sb("b_all", [P, NCH * CQ], F32)
        adj_sb = sb("adj_sb", [P, NCH, Q * CQ], I32)
        mask = sb("mask", [P, NCH, Q * CQ], BF16)
        wgt = sb("wgt", [P, NCH, Q, CQ], F32)
        wT = sb("wT", [P, 4, TS, P], F32)
        w_lo = sb("w_lo", [P, 4, TS, P], F16)
        gc = sb("gc", [P, 2, Q * ROWS], F32)
        neg_c = sb("neg_c", [P, Q * ROWS], F32)
        x_res = sb("x_res", [P, 2, D], F32)
        o_sb = sb("o_sb", [P, 2, D], F32)
        h_mean = sb("h_mean", [P, D], F32)
        no_nb = sb("no_nb", [P, 2], F32)
        den = sb("den", [P, 2], F32)
        r_den = sb("r_den", [P, 2], F32)
        h_f32 = sb("h_f32", [P, HR, HALF, D], F32)
        ident = sb("ident", [P, P], F32)
        same = sb("same", [P, B], F32)
        w12 = sb("w12", [P, 2], F32)
        b_col = sb("b_col", [P, 1], F32)
        b12 = sb("b12", [1, 2], F32)
        ones = sb("ones", [P, P], F32)
        cst = sb("cst", [P, 2], F32)
        f_col = sb("f_col", [P, ROWS, 2], F32)
        stats = sb("stats", [P, ROWS, 6], F32)
        mv = sb("mv", [P, ROWS, 2], F32)
        tiny = sb("tiny", [P, 8], F32)
        f2_rel = sb("f2_rel", [P, ROWS], F32)
        t_row = sb("t_row", [P, ROWS], F32)
        low = sb("low", [P, 2, ROWS], F32)
        var_eps = sb("var_eps", [P, ROWS], F32)
        minus_half = sb("minus_half", [P, TS], F32)
        rstd = sb("rstd", [P, ROWS], F32)
        D_big = sb("D_big", [P, ROWS], F32)
        D_inv = sb("D_inv", [P, ROWS], F32)
        D_parts = sb("D_parts", [P, ROWS, 2], F16)
        D_inv_parts = sb("D_inv_parts", [P, ROWS, 2], F16)
        h_mul = sb("h_mul", [P, ROWS], F32)
        h_add = sb("h_add", [P, ROWS], F32)
        h_sum = sb("h_sum", [2, D], F32)

        rp = ctx.enter_context(nc.psum_tensor("rp", [P, 2, CQ], F32))
        acc = ctx.enter_context(nc.psum_tensor("acc", [P, 2, 512], F32))
        small = ctx.enter_context(nc.psum_tensor("small", [P, 2, 512], F32))
        t_ps = small[:, 0, :]
        hm_ps = small[:, 0, 0:D]
        cst_ps = small[:, 0, 0:2]
        U_ps = small[:, 1, 0:2 * FM]
        fm_ps = small[0:1, 1, 256:256 + P]
        F_ps = small[:, 1, 384:385]
        hs_ps = small[0:2, 1, 0:D]

        w_hi = wT[:, :, :, :].rearrange("p a t i -> p (a t i)").bitcast(BF16).rearrange(
            "p (a t i e) -> p a t i e", a=4, t=TS, e=2)[:, :, :, :, 1]

        mask_room = mask[:, 1, :].bitcast(F32)

        def matrix_room(i):
            return mask_room[:, D + i * P:D + (i + 1) * P]

        W_sb = mask_room[:, 0:D]
        quads = matrix_room(0)
        f2_of = matrix_room(1)
        b_rep = matrix_room(2)
        pick = mask_room[:, D + 3 * P:D + (3 + Q) * P].rearrange(
            "p (q i) -> p q i", q=Q)

        def in2_stage(k):
            slot = wgt[:, k // 2, :, :].rearrange("p g n -> p (g n)") if k < 4 else \
                adj_sb[:, (k - 4) // 2, :].bitcast(F32)
            return slot[:, (k % 2) * TS * D:(k % 2 + 1) * TS * D].rearrange("p (t d) -> p t d", d=D)

        def x_stage(k):
            strip_room = H[:, TS * k:TS * (k + 1), :, :].rearrange("p t a d -> p (t a d)").bitcast(F32)
            return strip_room[:, RAW:RAW + TS * D].rearrange("p (t d) -> p t d", d=D)

        W_rep = h_f32[:, 0, :, :].rearrange("p t d -> p (t d)").rearrange(
            "p (m a r) -> p m a r", m=FM, a=Q)
        V = h_f32[:, 1, :, :].rearrange("p t d -> p (t d)").rearrange(
            "p (m i) -> p m i", m=FM)
        in2T = wT[:, :, :, :].rearrange("p (a e) t i -> p a (e t i)", e=2).rearrange(
            "p a (m n) -> p a m n", m=FM)
        f_rows = w_lo[:, :, :, :].rearrange("p a t i -> p (a t i)").bitcast(F32)
        f_cols = wgt[:, 1, 0:2, :].rearrange("p g n -> p (g n)")

        w_loaded = sem("w_loaded")
        biases_loaded = sem("biases_loaded")
        in2_loaded = [sem(f"in2_loaded{i}") for i in range(NS)]
        xs_loaded = [sem(f"xs_loaded{i}") for i in range(NS)]
        zeroed = sem("zeroed")
        ident_ready = sem("ident_ready")
        quads_ready = sem("quads_ready")
        ones_ready = sem("ones_ready")
        b_rep_ready = sem("b_rep_ready")
        pick_ready = sem("pick_ready")
        w_rep_ready = sem("w_rep_ready")
        u_ps_ready = sem("u_ps_ready")
        cst_ps_ready = sem("cst_ps_ready")
        u_ready = sem("u_ready")
        in2T_ready = sem("in2T_ready")
        f_done = sem("f_done")
        f_rows_ready = sem("f_rows_ready")
        f2_of_ready = sem("f2_of_ready")
        dve_step = sem("dve_step")
        f_max_part = sem("f_max_part")
        fm_ps_ready = sem("fm_ps_ready")
        f_max_ready = sem("f_max_ready")
        F_ps_ready = sem("F_ps_ready")
        f2_rel_ready = sem("f2_rel_ready")
        f_offset_ready = sem("f_offset_ready")
        b_ps_ready = sem("b_ps_ready")
        b_ready = sem("b_ready")
        low_ready = sem("low_ready")
        t_ps_ready = sem("t_ps_ready")
        gc_exp = sem("gc_exp")
        gc_ready = sem("gc_ready")
        D_exp = sem("D_exp")
        stats_ready = sem("stats_ready")
        var_ready = sem("var_ready")
        rstd_ready = sem("rstd_ready")
        h_affine_ready = sem("h_affine_ready")
        h_ready = sem("h_ready")
        hi_ready = sem("hi_ready")
        lo_ready = sem("lo_ready")
        h_sum_done = sem("h_sum_done")
        h_sum_ready = sem("h_sum_ready")
        h_mean_ps_ready = sem("h_mean_ps_ready")
        adj_loaded = [sem(f"adj_loaded{n}") for n in range(NS)]
        m_ready = sem("m_ready")
        r_ready = sem("r_ready")
        p_ready = sem("p_ready")
        t_ready = sem("t_ready")
        lo_split = sem("lo_split")
        mm_done = sem("mm_done")
        x_loaded = [sem(f"x_loaded{i}") for i in range(2)]
        fin_step = sem("fin_step")
        o_ready = sem("o_ready")
        o_stored = [sem(f"o_stored{i}") for i in range(2)]

        def row_tiles(eng, body, ahead=0):
            body(0, 0, 0)
            for v in range(ahead):
                body(2 * v + 1, 1, v)
                body(2 * v + 2, 0, v + 1)
            with eng.Fori(ahead, ROWS // 2 - 1) as v:
                body(2 * v + 1, 1, v)
                body(2 * v + 2, 0, v + 1)
            body(ROWS - 1, 1, ROWS // 2 - 1)

        def is_row(I, n):
            return type(I) is int and I == n

        block = ctx.enter_context(nc.Block())

        def load_strip(eng, stage, source, k, signal, quadrants):
            for q in quadrants:
                eng.dma_start(stage[B * q:B * (q + 1), :, :], source[k // SC, k % SC, q]).then_inc(signal, 16)

        def load_adj(eng, I, n):
            c, g = divmod(n, Q)
            eng.dma_start(adj_sb[:, c, g * CQ:(g + 1) * CQ], adj_q[I, g, c]).then_inc(adj_loaded[n], 16)

        def first_loads(eng, quadrants):
            for k in range(NS):
                load_strip(eng, in2_stage(k), in2_q, k, in2_loaded[k], quadrants)
                if k == SC - 1:
                    load_strip(eng, x_stage(0), x_q, 0, xs_loaded[0], quadrants)
            for k in range(1, 3):
                load_strip(eng, x_stage(k), x_q, k, xs_loaded[k], quadrants)

        @block.sync
        def _(sp):
            sp.dma_start(W_sb[:, :], W).then_inc(w_loaded, 16)
            sp.dma_start(w12[:, 0:1], w1.rearrange("(h o) -> h o", o=1)).then_inc(w_loaded, 16)
            sp.dma_start(w12[:, 1:2], w2.rearrange("(h o) -> h o", o=1)).then_inc(w_loaded, 16)
            first_loads(sp, (0, 1))
            sp.wait_ge(in2T_ready, 2 * 6)
            for n in range(Q):
                load_adj(sp, 0, n)
            load_strip(sp, x_stage(3), x_q, 3, xs_loaded[3], range(Q))
            sp.wait_ge(in2T_ready, 2 * 8)
            for n in range(Q, 2 * Q):
                load_adj(sp, 0, n)
            for k in range(4, NS):
                load_strip(sp, x_stage(k), x_q, k, xs_loaded[k], range(Q))
            for i in range(2):
                sp.dma_start(x_res[:, i, :], x_rows[i]).then_inc(x_loaded[i], 16)

            def body(I, par, half):
                for n in range(NS):
                    if not is_row(I, ROWS - 1):
                        sp.wait_ge(m_ready, 8 * I + (n + 1))
                        load_adj(sp, I + 1, n)
                    if n == 6 and not (is_row(I, 0) or is_row(I, 1)):
                        sp.wait_ge(o_ready, I - 1)
                        sp.dma_start(out_rows[I - 2], o_sb[:, par, :]).then_inc(o_stored[par], 16)
                        sp.dma_start(x_res[:, par, :], x_rows[I]).then_inc(x_loaded[par], 16)

            row_tiles(sp, body, ahead=1)
            for i in range(2):
                sp.wait_ge(o_ready, ROWS - 1 + i)
                sp.dma_start(out_rows[ROWS - 2 + i], o_sb[:, i, :]).then_inc(o_stored[i], 16)
            for i in range(2):
                sp.wait_ge(o_stored[i], 16 * ROWS // 2)

        @block.gpsimd
        def _(pool):
            nc.gpsimd.memset(ident[:, :], 0.0).then_inc(zeroed, 1)
            nc.gpsimd.memset(minus_half[:, :], -0.5).then_inc(zeroed, 1)
            pool.wait_ge(zeroed, 2)
            nc.gpsimd.affine_select(out=ident[:, :], in_=ident[:, :], compare_op=ALU.not_equal, fill=1.0, base=0,
                                    pattern=[[-1, P]], channel_multiplier=1).then_inc(ident_ready, 1)

            def rstds(k):
                pool.wait_ge(var_ready, 2 * k + 2)
                nc.gpsimd.tensor_tensor(rstd[:, TS * k:TS * (k + 1)], var_eps[:, TS * k:TS * (k + 1)],
                                        minus_half[:, :], ALU.pow).then_inc(rstd_ready, 1)

            def low_of_values(n):
                pool.wait_ge(h_ready, HALF * (n + 1))
                pool.wait_ge(hi_ready, n + 1)
                nc.gpsimd.tensor_tensor(H[:, HALF * n:HALF * (n + 1), 1, 0:D], h_f32[:, n % HR, :, :],
                                        H[:, HALF * n:HALF * (n + 1), 0, 0:D], ALU.subtract).then_inc(lo_ready, 1)

            def low_of_weights(I, k):
                pool.wait_ge(t_ready, 8 * I + (k + 1))
                nc.gpsimd.tensor_tensor(w_lo[:, k % 4, :, :], wT[:, k % 4, :, :], w_hi[:, k % 4, :, :],
                                        ALU.subtract).then_inc(lo_split, 1)

            rstds(0)
            rstds(1)
            for k in range(NS):
                low_of_values(2 * k)
                if k >= 1:
                    low_of_weights(0, k - 1)
                if k + 2 < NS:
                    rstds(k + 2)
                low_of_values(2 * k + 1)
            low_of_weights(0, NS - 1)
            with pool.Fori(1, ROWS) as I:
                for k in range(NS):
                    low_of_weights(I, k)

        @block.scalar
        def _(act):
            act.dma_start(b_col[:, :], b.rearrange("(h o) -> h o", o=1)).then_inc(biases_loaded, 16)
            act.dma_start(b12[:, 0:1], b1.rearrange("(h o) -> h o", o=1)).then_inc(biases_loaded, 16)
            act.dma_start(b12[:, 1:2], b2.rearrange("(h o) -> h o", o=1)).then_inc(biases_loaded, 16)
            first_loads(act, (2, 3))

            def f_to_sbuf(c):
                act.wait_ge(f_done, SC * (c + 1))
                nc.scalar.copy(f_rows[:, c * CQ:(c + 1) * CQ], rp[:, c, :]).then_inc(f_rows_ready, 1)

            def b_of_chunk(c):
                act.wait_ge(b_ps_ready, c + 1)
                nc.scalar.activation(b_all[:, c * CQ:(c + 1) * CQ], rp[:, c, :], ACT.Exp, scale=1.0 - SLOPE,
                                     bias=tiny[:, 3:4]).then_inc(b_ready, 1)

            def relu_part(I, g, c):
                nc.scalar.activation(rp[:, g % 2, :], b_all[:, c * CQ:(c + 1) * CQ], ACT.Relu,
                                     scale=gc[:, 0, bass.ds(Q * I + g, 1)],
                                     bias=neg_c[:, bass.ds(Q * I + g, 1)]).then_inc(r_ready, 1)

            def mask_part(I, g, c):
                act.wait_ge(adj_loaded[Q * c + g], 16 * I + 16)
                nc.scalar.activation(mask[:, c, g * CQ:(g + 1) * CQ], adj_sb[:, c, g * CQ:(g + 1) * CQ], ACT.Relu,
                                     scale=W_SCALE).then_inc(m_ready, 1)

            def values(n):
                act.wait_ge(h_affine_ready, n // 2 + 1)
                if n >= HR:
                    act.wait_ge(hi_ready, n - HR + 1)
                    act.wait_ge(lo_ready, n - HR + 1)
                for t in range(HALF):
                    j = HALF * n + t
                    nc.scalar.activation(h_f32[:, n % HR, t, :], x_stage(n // 2)[:, j % TS, :], ACT.Relu,
                                         scale=h_mul[:, j:j + 1], bias=h_add[:, j:j + 1]).then_inc(h_ready, 1)

            f_to_sbuf(0)
            f_to_sbuf(1)
            for g in range(Q):
                mask_part(0, g, 0)
            act.wait_ge(f_offset_ready, 1)
            b_of_chunk(0)
            act.wait_ge(f2_rel_ready, 1)
            nc.scalar.activation(D_big[:, :], f2_rel[:, :], ACT.Exp, scale=SLOPE).then_inc(D_exp, 1)
            nc.scalar.activation(D_inv[:, :], f2_rel[:, :], ACT.Exp, scale=-SLOPE).then_inc(D_exp, 1)
            b_of_chunk(1)
            act.wait_ge(t_ps_ready, 1)
            for kind in range(2):
                nc.scalar.activation(gc[:, kind, :].rearrange("p (c q m) -> p q c m", c=NCH, q=Q),
                                     t_ps.rearrange("p (q e c m) -> p q e c m", q=Q, e=2, c=NCH)[:, :, kind],
                                     ACT.Exp).then_inc(gc_exp, 1)
            act.wait_ge(gc_ready, 1)
            act.wait_ge(b_ready, NCH)
            for n in range(5):
                if n == 4:
                    mask_part(0, 0, 1)
                if n >= 2:
                    act.wait_ge(p_ready, n - 1)
                relu_part(0, n % Q, n // Q)
                if n < 2:
                    values(n)

            def masks_of(I, u):
                if is_row(I, 0):
                    return ((5, 6), (7, 8), (9,), (10, 11), (12,), (13,), (14,), (15,))[u]
                return () if is_row(I, ROWS - 1) else (8 + u,)

            def body(I):
                for u in range(NS):
                    c, g = divmod(u, Q)
                    if is_row(I, 0) and u + 1 < NS:
                        values(2 * u + 2)
                    pieces = masks_of(I, u)
                    if g == 3 or is_row(I, 0):
                        for m in pieces:
                            mask_part(I + m // NS, m % Q, m % NS // Q)
                    n = u + 5
                    if n < 2 * Q:
                        act.wait_ge(p_ready, 8 * I + (n - 1))
                        act.nop(nofuse=True)
                        relu_part(I, n % Q, n // Q)
                    elif not is_row(I, ROWS - 1):
                        act.wait_ge(p_ready, 8 * I + (n - 1))
                        act.nop(nofuse=True)
                        relu_part(I + 1, n % Q, n // Q - NCH)
                    if is_row(I, 0) and u + 1 < NS:
                        values(2 * u + 3)
                    if g < 3 and not is_row(I, 0):
                        for m in pieces:
                            mask_part(I + 1, m % Q, m % NS // Q)

            body(0)
            with act.Fori(1, ROWS - 2) as I:
                body(I)
            body(ROWS - 2)
            body(ROWS - 1)

        @block.vector
        def _(dve):
            steps = [0]

            def then_wait(ins):
                steps[0] += 1
                ins.then_inc(dve_step, 1)
                dve.wait_ge(dve_step, steps[0])

            nc.vector.memset(ones[:, :], 1.0).then_inc(ones_ready, 1)
            then_wait(nc.vector.memset(quads[:, :], 0.0))
            for q in range(Q):
                nc.vector.memset(quads[B * q:B * (q + 1), B * q:B * (q + 1)], 1.0).then_inc(quads_ready, 1)
            dve.wait_ge(w_loaded, 3 * 16)
            nc.vector.tensor_copy(W_rep[:, :, :, :], W_sb[:, :].rearrange("p (m r) -> p m r", m=FM).unsqueeze(2)
                                  .broadcast_to([P, FM, Q, B])).then_inc(w_rep_ready, 1)
            dve.wait_ge(ones_ready, 1)
            dve.wait_ge(biases_loaded, 3 * 16)
            nc.vector.tensor_scalar(b_rep[:, :], ones[:, :], b_col[:, 0:1], None, ALU.mult).then_inc(b_rep_ready, 1)

            def turn_in2(k):
                dve.wait_ge(in2_loaded[k], 64)
                if k >= 2:
                    dve.wait_ge(f_done, k - 1)
                for e in range(2):
                    nc.vector.transpose(in2T[:, k % 2, :, :].rearrange("p m (t s) -> p t m s", t=TS)[
                                            :, HALF * e:HALF * (e + 1), :, :],
                                        in2_stage(k)[:, HALF * e:HALF * (e + 1), :]).then_inc(in2T_ready, 1)

            turn_in2(0)
            dve.wait_ge(u_ps_ready, 1)
            for a in range(Q):
                nc.vector.tensor_scalar(V[:, :, B * a:B * (a + 1)].rearrange("p m (o v) -> p m o v", o=2),
                                        U_ps.rearrange("p (m o) -> p m o", m=FM).unsqueeze(3)
                                        .broadcast_to([P, FM, 2, B // 2]),
                                        quads[:, B * a:B * a + 1], None, ALU.mult).then_inc(u_ready, 1)
            dve.wait_ge(cst_ps_ready, 1)
            nc.vector.tensor_copy(cst[:, :], cst_ps).then_inc(u_ready, 1)
            dve.wait_ge(ident_ready, 1)
            turn_in2(1)
            for q in range(Q):
                nc.vector.tensor_copy(pick[:, q, :].rearrange("p (a r) -> p a r", a=Q),
                                      ident[:, B * q:B * (q + 1)].unsqueeze(1).broadcast_to([P, Q, B])
                                      ).then_inc(pick_ready, 1)
            nc.vector.tensor_reduce(same[:, :], ident[:, :].rearrange("p (q s) -> p s q", q=Q), AX.X,
                                    ALU.add).then_inc(pick_ready, 1)
            dve.wait_ge(pick_ready, Q + 1)
            nc.vector.tensor_scalar(f2_of[:, :], quads[:, :], same[:, B // 2:B // 2 + 1], None,
                                    ALU.mult).then_inc(f2_of_ready, 1)

            def chunk_f(c):
                at = slice(c * ROWS // NCH, (c + 1) * ROWS // NCH)
                dve.wait_ge(f_rows_ready, c + 1)
                dve.wait_ge(in2T_ready, 2 * SC)
                then_wait(nc.vector.transpose(f_cols[:, c * CQ:(c + 1) * CQ], f_rows[:, c * CQ:(c + 1) * CQ]))
                then_wait(nc.vector.tensor_copy(f_col[:, at, :], f_cols[:, c * CQ:(c + 1) * CQ].rearrange(
                    "p (j o v) -> p j o v", o=2, v=B // 2)[:, :, :, 0]))
                then_wait(nc.vector.reduce_max(tiny[:, 6 + c:7 + c], f_col[:, at, 1], AX.X))
                if c == 1:
                    nc.vector.tensor_tensor(tiny[:, 0:1], tiny[:, 6:7], tiny[:, 7:8], ALU.max).then_inc(f_max_part, 1)

            def raw_stats(first, end):
                for j in range(first, end):
                    if j == first or j % TS == 0:
                        dve.wait_ge(xs_loaded[j // TS], 64)
                    nc.vector.bn_stats(out=stats[:, j, :], in_=x_stage(j // TS)[:, j % TS, :]).then_inc(stats_ready, 1)

            def mean_var(n):
                at = slice(HALF * n, HALF * (n + 1))
                dve.wait_ge(stats_ready, HALF * (n + 1))
                for j in range(HALF * n, HALF * (n + 1)):
                    ins = nc.vector.bn_aggr(out=mv[:, j, :], in_=stats[:, j, :])
                then_wait(ins)
                nc.vector.tensor_scalar(var_eps[:, at], mv[:, at, 1], EPS, None, ALU.add).then_inc(var_ready, 1)

            def half_stats(n):
                raw_stats(HALF * n, HALF * (n + 1))
                mean_var(n)

            for k in range(2, NS):
                if k == 7:
                    chunk_f(0)
                turn_in2(k)
                if 4 <= k < 7:
                    raw_stats(3 * (k - 4), 3 * (k - 3))
            raw_stats(9, 16)
            for n in range(4):
                mean_var(n)
            raw_stats(16, 20)
            chunk_f(1)
            dve.wait_ge(fm_ps_ready, 1)
            nc.vector.reduce_max(tiny[0:1, 1:2], fm_ps, AX.X).then_inc(f_max_ready, 1)
            dve.wait_ge(u_ready, Q + 1)
            then_wait(nc.vector.tensor_tensor(tiny[:, 4:5], cst[:, 0:1], cst[:, 1:2], ALU.add))
            dve.wait_ge(F_ps_ready, 1)
            nc.vector.tensor_scalar(tiny[:, 3:4], F_ps, SLOPE - 1.0, None, ALU.mult).then_inc(f_offset_ready, 1)
            then_wait(nc.vector.tensor_copy(tiny[:, 2:3], F_ps))
            then_wait(nc.vector.tensor_tensor(tiny[:, 5:6], tiny[:, 4:5], tiny[:, 2:3], ALU.add))
            then_wait(nc.vector.tensor_scalar(t_row[:, :], f_col[:, :, 0], tiny[:, 5:6], 1.0 - SLOPE, ALU.add, ALU.mult))
            nc.vector.tensor_scalar(low[:, 0, :], t_row[:, :], 0.0, None, ALU.min).then_inc(low_ready, 1)
            nc.vector.tensor_scalar(low[:, 1, :], t_row[:, :], -1.0, 0.0, ALU.mult, ALU.min).then_inc(low_ready, 1)
            nc.vector.tensor_scalar(f2_rel[:, :], f_col[:, :, 1], tiny[:, 2:3], None,
                                    ALU.subtract).then_inc(f2_rel_ready, 1)

            def affine(k):
                at = slice(TS * k, TS * (k + 1))
                dve.wait_ge(rstd_ready, k + 1)
                then_wait(nc.vector.tensor_tensor(h_mul[:, at], rstd[:, at], D_big[:, at], ALU.mult))
                nc.vector.scalar_tensor_tensor(out=h_add[:, at], in0=mv[:, at, 0], scalar=-1.0, in1=h_mul[:, at],
                                               op0=ALU.mult, op1=ALU.mult).then_inc(h_affine_ready, 1)

            def high_of_values(n):
                at = slice(HALF * n, HALF * (n + 1))
                dve.wait_ge(h_ready, HALF * (n + 1))
                nc.vector.tensor_copy(H[:, at, :, D], D_parts[:, at, :])
                nc.vector.tensor_copy(H[:, at, 0, 0:D], h_f32[:, n % HR, :, :]).then_inc(hi_ready, 1)

            def weights(I, g, c):
                dve.wait_ge(r_ready, 8 * I + (Q * c + g + 1))
                dve.wait_ge(m_ready, 8 * I + (Q * c + g + 1))
                nc.vector.scalar_tensor_tensor(out=wgt[:, c, g, :], in0=rp[:, g % 2, :],
                                               scalar=gc[:, 1, bass.ds(Q * I + g, 1)],
                                               in1=mask[:, c, g * CQ:(g + 1) * CQ], op0=ALU.add,
                                               op1=ALU.min).then_inc(p_ready, 1)

            def turn(I, k):
                c, s = divmod(k, SC)
                dve.wait_ge(p_ready, 8 * I + Q * (c + 1))
                if not (is_row(I, 0) and k < 4):
                    dve.wait_ge(mm_done, 8 * I + (k - 3) if k >= 3 else 8 * I - (3 - k))
                nc.vector.transpose(wT[:, k % 4, :, :].rearrange("p t (g r) -> p g t r", g=Q),
                                    wgt[:, c, :, s * SQ:(s + 1) * SQ]).then_inc(t_ready, 1)

            def finish_0(I, par, half):
                dve.wait_ge(mm_done, 8 * I + 8)
                nc.vector.tensor_scalar(no_nb[:, par:par + 1], acc[:, par, D:DV], 0.0, None,
                                        ALU.is_equal).then_inc(fin_step, 1)

            def finish_1(I, par, half):
                dve.wait_ge(fin_step, 4 * I + 1)
                nc.vector.tensor_tensor(den[:, par:par + 1], acc[:, par, D:DV], no_nb[:, par:par + 1],
                                        ALU.add).then_inc(fin_step, 1)

            def finish_2(I, par, half):
                dve.wait_ge(fin_step, 4 * I + 2)
                nc.vector.reciprocal(r_den[:, par:par + 1], den[:, par:par + 1]).then_inc(fin_step, 1)

            def finish_3(I, par, half):
                dve.wait_ge(fin_step, 4 * I + 3)
                dve.wait_ge(x_loaded[par], 16 * half + 16)
                nc.vector.scalar_tensor_tensor(out=x_res[:, par, :], in0=acc[:, par, 0:D], scalar=r_den[:, par:par + 1],
                                               in1=x_res[:, par, :], op0=ALU.mult, op1=ALU.add).then_inc(fin_step, 1)

            def finish_4(I, par, half):
                dve.wait_ge(fin_step, 4 * I + 4)
                dve.wait_ge(o_stored[par], 16 * half)
                nc.vector.scalar_tensor_tensor(out=o_sb[:, par, :], in0=h_mean[:, :], scalar=no_nb[:, par:par + 1],
                                               in1=x_res[:, par, :], op0=ALU.mult, op1=ALU.add).then_inc(o_ready, 1)

            dve.wait_ge(D_exp, 2)
            then_wait(nc.vector.tensor_scalar(D_big[:, :], D_big[:, :], H_SCALE, None, ALU.mult))
            affine(0)
            mean_var(4)
            dve.wait_ge(gc_exp, 2)
            then_wait(nc.vector.tensor_scalar(gc[:, :, :], gc[:, :, :], W_SCALE, None, ALU.mult))
            nc.vector.tensor_scalar(neg_c[:, :], gc[:, 1, :], -1.0, None, ALU.mult).then_inc(gc_ready, 1)
            nc.vector.tensor_copy(D_parts[:, :, 0], D_big[:, :])
            then_wait(nc.vector.tensor_copy(D_inv_parts[:, :, 0], D_inv[:, :]))
            nc.vector.tensor_tensor(D_parts[:, :, 1], D_big[:, :], D_parts[:, :, 0], ALU.subtract)
            then_wait(nc.vector.tensor_tensor(D_inv_parts[:, :, 1], D_inv[:, :], D_inv_parts[:, :, 0], ALU.subtract))
            weights(0, 0, 0)
            affine(1)
            high_of_values(0)
            weights(0, 1, 0)
            half_stats(5)
            high_of_values(1)
            weights(0, 2, 0)
            weights(0, 3, 0)

            def body(I, par, half):
                def finish_previous(step):
                    if not is_row(I, 0):
                        step(I - 1, 1 - par, half - 1 + par)

                def next_weights(g, c):
                    if c == 0:
                        weights(I, g, 1)
                    elif not is_row(I, ROWS - 1):
                        weights(I + 1, g, 0)

                for u in range(NS):
                    c, g = divmod(u, Q)
                    if g == 0:
                        turn(I, u)
                        if not is_row(I, 0) or c == 1:
                            dve.wait_ge(t_ready, 8 * I + u)
                        if u == 4:
                            finish_previous(finish_1)
                        next_weights(g, c)
                        if u == 4:
                            finish_previous(finish_2)
                    else:
                        next_weights(g, c)
                        if u == 5:
                            finish_previous(finish_3)
                        turn(I, u)
                        if u == 3:
                            finish_previous(finish_0)
                        if u == 5:
                            finish_previous(finish_4)
                    if is_row(I, 0):
                        if u + 1 < NS:
                            high_of_values(2 * u + 2)
                        if u + 3 < NS:
                            half_stats(2 * u + 6)
                        if u + 1 < NS:
                            high_of_values(2 * u + 3)
                        if u + 2 < NS:
                            affine(u + 2)
                        if u + 3 < NS:
                            half_stats(2 * u + 7)
                    if is_row(I, 1) and u == 1:
                        dve.wait_ge(h_sum_done, 1)
                        nc.vector.tensor_scalar(h_sum[:, :], hs_ps, 1.0 / (H_SCALE * N), None,
                                                ALU.mult).then_inc(h_sum_ready, 1)
                    if is_row(I, 1) and u == 2:
                        dve.wait_ge(h_mean_ps_ready, 1)
                        then_wait(nc.vector.tensor_copy(h_mean[:, :], hm_ps))

            row_tiles(dve, body, ahead=1)
            for step in (finish_0, finish_1, finish_2, finish_3, finish_4):
                step(ROWS - 1, 1, ROWS // 2 - 1)

        @block.tensor
        def _(pe):
            pe.wait_ge(w_loaded, 3 * 16)
            pe.wait_ge(w_rep_ready, 1)
            for m in range(FM):
                mm = pe.matmul(U_ps[:, 2 * m:2 * (m + 1)], W_rep[:, m, :, :], w12[:, :],
                               start=True, stop=True)
            mm.then_inc(u_ps_ready, 1)
            pe.wait_ge(b_rep_ready, 1)
            pe.wait_ge(biases_loaded, 3 * 16)
            pe.matmul(cst_ps, b_rep[:, :], w12[:, :], start=True, stop=False)
            pe.matmul(cst_ps, ones[0:1, :], b12[:, :], start=False, stop=True).then_inc(cst_ps_ready, 1)

            def f_of_strip(k):
                pe.wait_ge(in2T_ready, 2 * (k + 1))
                for m in range(FM):
                    mm = pe.matmul(rp[:, k // SC, SQ * (k % SC):SQ * (k % SC + 1)], V[:, m, :], in2T[:, k % 2, m, :],
                                   start=(m == 0), stop=(m == FM - 1))
                mm.then_inc(f_done, 1)

            def b_exponents(c):
                pe.wait_ge(f_rows_ready, c + 1)
                for n in range(2):
                    mm = pe.matmul(rp[:, c, n * 512:(n + 1) * 512], f2_of[:, :],
                                   f_rows[:, c * CQ + n * 512:c * CQ + (n + 1) * 512], start=True, stop=True)
                mm.then_inc(b_ps_ready, 1)

            pe.wait_ge(u_ready, Q)
            for k in range(NS):
                if k == 6:
                    pe.wait_ge(f2_of_ready, 1)
                    b_exponents(0)
                f_of_strip(k)
            b_exponents(1)
            pe.wait_ge(ident_ready, 1)
            pe.wait_ge(f_max_part, 1)
            pe.wait_ge(u_ready, Q + 1)
            pe.transpose(fm_ps, tiny[:, 0:1], ident[:, :]).then_inc(fm_ps_ready, 1)
            pe.wait_ge(f_max_ready, 1)
            pe.matmul(F_ps, ones[0:1, :], tiny[0:1, 1:2], start=True, stop=True).then_inc(F_ps_ready, 1)
            pe.wait_ge(low_ready, 2)
            pe.wait_ge(pick_ready, Q + 1)
            for q in range(Q):
                mm = pe.matmul(t_ps[:, 2 * ROWS * q:2 * ROWS * (q + 1)], pick[:, q, :],
                               low[:, :, :].rearrange("p e j -> p (e j)"), start=True, stop=True)
            mm.then_inc(t_ps_ready, 1)
            def products(I, par, k):
                pe.wait_ge(t_ready, 8 * I + (k + 1))
                for t in range(TS):
                    j = TS * k + t
                    for part in range(2):
                        pe.matmul(acc[:, par, 0:DV], w_hi[:, k % 4, t, :], H[:, j, part, 0:DV],
                                  start=(j == 0 and part == 0), stop=False)
                pe.wait_ge(lo_split, 8 * I + (k + 1))
                for t in range(TS):
                    j = TS * k + t
                    mm = pe.matmul(acc[:, par, 0:DV], w_lo[:, k % 4, t, :], H[:, j, 0, 0:DV],
                                   start=False, stop=(j == ROWS - 1))
                mm.then_inc(mm_done, 1)

            def sum_of_values(k):
                for j in range(TS * k, TS * (k + 1)):
                    for part in range(2):
                        mm = pe.matmul(hs_ps, D_inv_parts[:, j, :], H[:, j, part, 0:D],
                                       start=(j == 0 and part == 0), stop=(j == ROWS - 1 and part == 1))
                return mm

            def body(I, par, half):
                for k in range(NS):
                    if k == NS - 1:
                        pe.wait_ge(o_ready, I)
                    if is_row(I, 0):
                        pe.wait_ge(hi_ready, 2 * k + 2)
                        pe.wait_ge(lo_ready, 2 * k + 2)
                    products(I, par, k)
                    if is_row(I, 0):
                        mm = sum_of_values(k)
                if is_row(I, 0):
                    mm.then_inc(h_sum_done, 1)
                    pe.wait_ge(h_sum_ready, 1)
                    pe.matmul(hm_ps, ones[0:2, :], h_sum[:, :], start=True, stop=True).then_inc(h_mean_ps_ready, 1)

            row_tiles(pe, body)


_INS = ["x", "adj", "L0_gnn_inlayer2", "L0_gnn_W", "L0_gnn_b", "L0_gnn_w1", "L0_gnn_b1", "L0_gnn_w2", "L0_gnn_b2"]


def kernel(**inputs):
    import numpy as np
    import concourse.bacc as bacc
    from concourse.bass_utils import run_bass_kernel_spmd

    nc = bacc.Bacc("TRN2", target_bir_lowering=False, num_devices=1)
    arrays, args = {}, []
    for name in _INS:
        a = np.ascontiguousarray(inputs[name])
        arrays[f"in_{name}_dram"] = a
        args.append(nc.dram_tensor(f"in_{name}_dram", a.shape, mybir.dt.from_np(a.dtype), kind="ExternalInput").ap())
    out = nc.dram_tensor("out_0_dram", inputs["x"].shape, F32, kind="ExternalOutput").ap()
    graph_attention(nc, *args, out)
    r = run_bass_kernel_spmd(nc, [arrays], core_ids=[0])
    return r.results[0]["out_0_dram"]
```
